# Optimizing a Trainium2 kernel written in Bass

```python
import numpy as np
import jax
import jax.numpy as jnp

def _softmax(x, axis=-1):
    return jax.nn.softmax(x, axis=axis)

def _gelu(x):
    return jax.nn.gelu(x, approximate=True)

def _silu(x):
    return jax.nn.silu(x)

def _sigmoid(x):
    return jax.nn.sigmoid(x)

def _layernorm(x, axis=-1, eps=1e-05):
    m = jnp.mean(x, axis=axis, keepdims=True)
    v = jnp.var(x, axis=axis, keepdims=True)
    return (x - m) / jnp.sqrt(v + eps)

def _scatter_add(tgt, idx, src, axis=0):
    return tgt.at[idx].add(src)

def _segment_sum(src, seg, n):
    return jax.ops.segment_sum(src, seg, n)
kernel_name = 'mk_perceiver_d1_seqx_r2_b2b66c'

def setup_inputs(seed: int=0):
    np.random.seed(seed)
    _w = jnp.asarray

    def _rec_inputs():
        import jax
        import jax.numpy as jnp
        _rk = jax.random.key(seed)
        x = -0.0002928 + 1 * jax.random.normal(jax.random.fold_in(_rk, 1), (1, 256, 512), jnp.float32)
        _lenS = 256 - jax.random.randint(jax.random.fold_in(_rk, 7), (1,), 0, max(1, 256 // 4) + 1, jnp.int32)
        _lenS2 = 25088 - jax.random.randint(jax.random.fold_in(_rk, 8), (1,), 0, max(1, 25088 // 4) + 1, jnp.int32)
        _ctx_1024P = jax.random.normal(jax.random.fold_in(_rk, 11), (1, 16, 512), jnp.float32)
        _ctx_1024c = jax.random.dirichlet(jax.random.fold_in(_rk, 511), 0.3 * jnp.ones((16,), jnp.float32), (1, 25088))
        _ctx_1024t = jnp.einsum('bsk,bkd->bsd', _ctx_1024c, _ctx_1024P)
        _ctx_1024t = _ctx_1024t * jax.lax.rsqrt(jnp.mean(jnp.square(_ctx_1024t)) + 1e-12) * 0.953939
        ctx_1024 = -1.39393e-06 + 0.999914 * (_ctx_1024t + 0.3 * jax.random.normal(jax.random.fold_in(_rk, 611), (1, 25088, 512), jnp.float32))
        return (x, ctx_1024)
    x, ctx_1024 = _rec_inputs()

    def _L0_xattn_setup():
        import jax, jax.numpy as jnp
        import numpy as np
        EMBED_DIM = 512
        NUM_HEADS = 16
        HEAD_DIM = EMBED_DIM // NUM_HEADS
        key = jax.random.key(seed)
        ks = jax.random.split(key, 7)
        B, S, E = (2, 1024, EMBED_DIM)
        bound = float(np.sqrt(6.0 / (E + E)))
        mkw = lambda k: jax.random.uniform(k, (E, E), jnp.float32, -bound, bound)
        return {'query': jax.random.normal(ks[0], (B, S, E), jnp.float32), 'key': jax.random.normal(ks[1], (B, S, E), jnp.float32), 'value': jax.random.normal(ks[2], (B, S, E), jnp.float32), 'Wq': mkw(ks[3]), 'Wk': mkw(ks[4]), 'Wv': mkw(ks[5]), 'Wo': mkw(ks[6])}
    _L0_xattn_all = _L0_xattn_setup()
    _L0_xattn_in = {k: v for k, v in _L0_xattn_all.items() if k in ('Wq', 'Wk', 'Wv', 'Wo')}
    del _L0_xattn_all

    def _L0_attn_setup():
        import jax, jax.numpy as jnp
        import numpy as np
        D_MODEL = 512
        D_QK = 512
        NUM_HEADS = 16
        HEAD_DIM = D_QK // NUM_HEADS
        V_DIM = D_MODEL // NUM_HEADS
        B, S = (2, 1024)
        key = jax.random.key(seed)
        ks = jax.random.split(key, 9)
        sc = 0.02
        return {'x': jax.random.normal(ks[0], (B, S, D_MODEL), dtype=jnp.float32), 'Wqk': jax.random.normal(ks[1], (D_MODEL, 2 * D_QK), dtype=jnp.float32) * sc, 'bqk': jax.random.normal(ks[2], (2 * D_QK,), dtype=jnp.float32) * sc, 'Wv': jax.random.normal(ks[3], (D_MODEL, D_MODEL), dtype=jnp.float32) * sc, 'bv': jax.random.normal(ks[4], (D_MODEL,), dtype=jnp.float32) * sc, 'Wn': jax.random.normal(ks[5], (D_MODEL, NUM_HEADS), dtype=jnp.float32) * sc, 'bn': jax.random.normal(ks[6], (NUM_HEADS,), dtype=jnp.float32) * sc, 'Wo': jax.random.normal(ks[7], (D_MODEL, D_MODEL), dtype=jnp.float32) * sc, 'bo': jax.random.normal(ks[8], (D_MODEL,), dtype=jnp.float32) * sc}
    _L0_attn_all = _L0_attn_setup()
    _L0_attn_in = {k: v for k, v in _L0_attn_all.items() if k in ('Wqk', 'bqk', 'Wv', 'bv', 'Wn', 'bn', 'Wo', 'bo')}
    del _L0_attn_all

    def _L0_ffn_setup():
        import jax, jax.numpy as jnp
        import numpy as np
        D_IN, D_HID = (512, 2048)

        def _ternary(key, shape):
            return jax.random.randint(key, shape, -1, 2).astype(jnp.float32)

        def _tlin(x, w, s):
            return jnp.einsum('bsi,oi->bso', x, w) * s
        key = jax.random.key(seed)
        ks = jax.random.split(key, 12)
        inv = lambda fan: 1.0 / np.sqrt(fan).astype(np.float32)
        return {'x': jax.random.normal(ks[0], (4, 1024, D_IN), dtype=jnp.float32), 'w1_w': _ternary(ks[1], (D_HID, D_IN)), 'w1_s': jax.random.uniform(ks[2], (D_HID,), dtype=jnp.float32) * inv(D_IN), 'w2_w': _ternary(ks[3], (D_HID, D_IN)), 'w2_s': jax.random.uniform(ks[4], (D_HID,), dtype=jnp.float32) * inv(D_IN), 'h1_w': _ternary(ks[5], (D_HID, D_HID)), 'h1_s': jax.random.uniform(ks[6], (D_HID,), dtype=jnp.float32) * inv(D_HID), 'h2_w': _ternary(ks[7], (D_HID, D_HID)), 'h2_s': jax.random.uniform(ks[8], (D_HID,), dtype=jnp.float32) * inv(D_HID), 'w3_w': _ternary(ks[9], (D_IN, D_HID)), 'w3_s': jax.random.uniform(ks[10], (D_IN,), dtype=jnp.float32) * inv(D_HID)}
    _L0_ffn_all = _L0_ffn_setup()
    _L0_ffn_in = {k: v for k, v in _L0_ffn_all.items() if k in ('w1_w', 'w1_s', 'w2_w', 'w2_s', 'h1_w', 'h1_s', 'h2_w', 'h2_s', 'w3_w', 'w3_s')}
    del _L0_ffn_all
    return {'x': x, 'ctx_1024': ctx_1024, 'L0_xattn_Wq': _L0_xattn_in['Wq'], 'L0_xattn_Wk': _L0_xattn_in['Wk'], 'L0_xattn_Wv': _L0_xattn_in['Wv'], 'L0_xattn_Wo': _L0_xattn_in['Wo'], 'L0_attn_Wqk': _L0_attn_in['Wqk'], 'L0_attn_bqk': _L0_attn_in['bqk'], 'L0_attn_Wv': _L0_attn_in['Wv'], 'L0_attn_bv': _L0_attn_in['bv'], 'L0_attn_Wn': _L0_attn_in['Wn'], 'L0_attn_bn': _L0_attn_in['bn'], 'L0_attn_Wo': _L0_attn_in['Wo'], 'L0_attn_bo': _L0_attn_in['bo'], 'L0_ffn_w1_w': _L0_ffn_in['w1_w'], 'L0_ffn_w1_s': _L0_ffn_in['w1_s'], 'L0_ffn_w2_w': _L0_ffn_in['w2_w'], 'L0_ffn_w2_s': _L0_ffn_in['w2_s'], 'L0_ffn_h1_w': _L0_ffn_in['h1_w'], 'L0_ffn_h1_s': _L0_ffn_in['h1_s'], 'L0_ffn_h2_w': _L0_ffn_in['h2_w'], 'L0_ffn_h2_s': _L0_ffn_in['h2_s'], 'L0_ffn_w3_w': _L0_ffn_in['w3_w'], 'L0_ffn_w3_s': _L0_ffn_in['w3_s']}

def reference(x, ctx_1024, L0_xattn_Wq, L0_xattn_Wk, L0_xattn_Wv, L0_xattn_Wo, L0_attn_Wqk, L0_attn_bqk, L0_attn_Wv, L0_attn_bv, L0_attn_Wn, L0_attn_bn, L0_attn_Wo, L0_attn_bo, L0_ffn_w1_w, L0_ffn_w1_s, L0_ffn_w2_w, L0_ffn_w2_s, L0_ffn_h1_w, L0_ffn_h1_s, L0_ffn_h2_w, L0_ffn_h2_s, L0_ffn_w3_w, L0_ffn_w3_s):
    import jax
    import jax.numpy as jnp

    def _L0_xattn_ref(query, key, value, Wq, Wk, Wv, Wo):
        import jax, jax.numpy as jnp
        import numpy as np
        EMBED_DIM = 512
        NUM_HEADS = 16
        HEAD_DIM = EMBED_DIM // NUM_HEADS
        B, L, E = query.shape
        H, D = (NUM_HEADS, HEAD_DIM)
        scale = D ** (-0.5)
        q = (query @ Wq.T).reshape(B, L, H, D) * scale
        k = (key @ Wk.T).reshape(B, -1, H, D)
        v = (value @ Wv.T).reshape(B, -1, H, D)
        scores = jax.nn.sigmoid(jnp.einsum('blhd,bshd->bhls', q, k))
        o = jnp.einsum('bhls,bshd->blhd', scores, v).reshape(B, L, E)
        return o @ Wo.T

    def _L0_attn_ref(x, Wqk, bqk, Wv, bv, Wn, bn, Wo, bo):
        import jax, jax.numpy as jnp
        import numpy as np
        D_MODEL = 512
        D_QK = 512
        NUM_HEADS = 16
        HEAD_DIM = D_QK // NUM_HEADS
        V_DIM = D_MODEL // NUM_HEADS
        B, S = (2, 1024)
        b, s, _ = x.shape
        qk = x @ Wqk + bqk
        v = x @ Wv + bv
        n = x @ Wn + bn
        qk = qk.reshape(b, s, 2, NUM_HEADS, HEAD_DIM)
        q, k = (qk[:, :, 0], qk[:, :, 1])
        v = v.reshape(b, s, NUM_HEADS, V_DIM)
        scores = jnp.einsum('bthd,bshd->bhts', q, k)
        mask = jnp.tril(jnp.ones((s, s), dtype=scores.dtype))
        n_exp = jnp.exp(jnp.transpose(n, (0, 2, 1)))
        attn = scores * mask / n_exp[:, :, :, None]
        ctx = jnp.einsum('bhts,bshd->bthd', attn, v)
        ctx = ctx.reshape(b, s, D_MODEL)
        return ctx @ Wo + bo

    def _L0_ffn_ref(x, w1_w, w1_s, w2_w, w2_s, h1_w, h1_s, h2_w, h2_s, w3_w, w3_s):
        import jax, jax.numpy as jnp
        import numpy as np
        D_IN, D_HID = (512, 2048)

        def _ternary(key, shape):
            return jax.random.randint(key, shape, -1, 2).astype(jnp.float32)

        def _tlin(x, w, s):
            return jnp.einsum('bsi,oi->bso', x, w) * s
        h = jax.nn.silu(_tlin(x, w1_w, w1_s)) * _tlin(x, w2_w, w2_s)
        h = jax.nn.gelu(_tlin(h, h1_w, h1_s), approximate=False)
        h = jax.nn.gelu(_tlin(h, h2_w, h2_s), approximate=False)
        return _tlin(h, w3_w, w3_s)
    x = x + _L0_xattn_ref(_layernorm(x, axis=-1), ctx_1024, ctx_1024, L0_xattn_Wq, L0_xattn_Wk, L0_xattn_Wv, L0_xattn_Wo)
    x = x + _L0_attn_ref(_layernorm(x, axis=-1), L0_attn_Wqk, L0_attn_bqk, L0_attn_Wv, L0_attn_bv, L0_attn_Wn, L0_attn_bn, L0_attn_Wo, L0_attn_bo)
    x = x + _L0_ffn_ref(_layernorm(x, axis=-1), L0_ffn_w1_w, L0_ffn_w1_s, L0_ffn_w2_w, L0_ffn_w2_s, L0_ffn_h1_w, L0_ffn_h1_s, L0_ffn_h2_w, L0_ffn_h2_s, L0_ffn_w3_w, L0_ffn_w3_s)
    return x

_drawn_inputs = setup_inputs


def setup_inputs(seed=0):
    import zlib

    import numpy as np

    out = dict(_drawn_inputs(seed))
    spreads = {}
    factors = {}
    for name, (base, spread) in spreads.items():
        noise = np.random.default_rng([zlib.crc32(name.encode()), seed]).standard_normal(out[name].shape)
        drawn = base * np.exp(spread * noise) if base else spread * noise
        out[name] = jnp.asarray(drawn.astype(out[name].dtype))
    for name, factor in factors.items():
        out[name] = (out[name] * factor).astype(out[name].dtype)
    return out
```

```python
from contextlib import ExitStack

import numpy as np

import concourse.bass as bass
from concourse import mybir

F32 = mybir.dt.float32
F32R = mybir.dt.float32r
BF16 = mybir.dt.bfloat16
ALU = mybir.AluOpType
ACT = mybir.ActivationFunctionType

P = 128
L = 256
E = 512
S = 25088
H = 16
D = E // H
HID = 2048
KE = E // P
KH = HID // P
LT = L // P
HG = P // D
G = H // HG
CH = 512
NC = S // CH
TC = CH // P
EPS = 1e-5
UNIT = KH * P
assert NC * CH == S and G == TC == KE


def f32(ap):
    return ap.bitcast(F32)


def layernorm(nc, dve, act_done, x, xn, stats, mv, link, ask_sqrt):
    for a in range(LT):
        link(nc.vector.bn_stats(stats[:, a, :], x[:, a, :]))
        link(nc.vector.bn_aggr(mv[:, a, 0:2], stats[:, a, :]))
    link(nc.vector.tensor_scalar_add(mv[:, :, 2:3], mv[:, :, 1:2], EPS))
    ask_sqrt()
    link(nc.vector.reciprocal(mv[:, :, 3:4], mv[:, :, 2:3]))
    for a in range(LT):
        last = nc.vector.tensor_scalar(xn[:, a, :], x[:, a, :], mv[:, a, 0:1], mv[:, a, 3:4],
                                       ALU.subtract, ALU.mult)
    return last


class Chain:

    def __init__(self, engine, sem):
        self.engine, self.sem, self.n = engine, sem, 0

    def __call__(self, instruction):
        self.n += 1
        instruction.then_inc(self.sem, 1)
        self.engine.wait_ge(self.sem, self.n)


def cross_attention(nc, x, ctxT, wqT, wkT, wvT, keep):
    ident, zeros, oT = keep["ident"], keep["zeros"], keep["oT"]
    with ExitStack() as stack:
        def sb(name, shape, dt=F32):
            return stack.enter_context(nc.sbuf_tensor(name, shape, dt))

        def sem(name):
            return stack.enter_context(nc.semaphore(name))

        wk_hi, wk_lo = sb("wk_hi", [P, KE, E], F32R), sb("wk_lo", [P, KE, E], F32R)
        wv_hi, wv_lo = sb("wv_hi", [P, KE, E], F32R), sb("wv_lo", [P, KE, E], F32R)
        raw = sb("ctx_raw", [P, KE, CH])
        c_hi, c_lo = sb("c_hi", [P, 2, KE, CH], F32R), sb("c_lo", [P, 2, KE, CH], F32R)
        kst = sb("k_stack", [P, 2, HG, G, CH], F32R)
        qst = sb("q_stack", [P, HG, G, L], F32R)
        v = sb("v", [P, 2, E])
        probs = sb("probs", [P, 2, G, HG * L])
        stats, mv = sb("ln_stats", [P, LT, 6]), sb("ln_mv", [P, LT, 4])
        wk_raw = probs[:, 0, 0:2, :].rearrange("p a b -> p (a b)").rearrange("p (k n) -> p k n", k=KE)
        wv_raw = probs[:, 0, 2:4, :].rearrange("p a b -> p (a b)").rearrange("p (k n) -> p k n", k=KE)
        wq_raw = probs[:, 1, 2:4, :].rearrange("p a b -> p (a b)").rearrange("p (k n) -> p k n", k=KE)
        x_sb = probs[:, 1, 0, :].rearrange("p (a n) -> p a n", a=LT)
        xn = probs[:, 1, 1, :].rearrange("p (a n) -> p a n", a=LT)
        xnT = v[:, :, :].rearrange("p a n -> p (a n)").rearrange("p (k l) -> p k l", k=KE)

        sc = [stack.enter_context(nc.psum_tensor(f"sc{i}", [P, HG * L], F32)) for i in range(2)]
        kp = stack.enter_context(nc.psum_tensor("kp", [P, CH], F32))
        vp = stack.enter_context(nc.psum_tensor("vp", [P, E], F32))
        acc = stack.enter_context(nc.psum_tensor("acc", [P, G, L], F32))

        x_loaded, wq_loaded = sem("x_loaded"), sem("wq_loaded")
        wk_loaded, wv_loaded = sem("wk_loaded"), sem("wv_loaded")
        ctx_loaded = sem("ctx_loaded")
        const_ready, const_step = sem("const_ready"), sem("const_step")
        dve_chain, sqrt_asked, sqrt_done = sem("dve_chain"), sem("sqrt_asked"), sem("sqrt_done")
        xn_ready, xnT_made, xnT_ready, q_made, q_ready = (
            sem("xn_ready"), sem("xnT_made"), sem("xnT_ready"), sem("q_made"), sem("q_ready"))
        wk_split, wv_split = sem("wk_split"), sem("wv_split")
        ctx_hi, ctx_split = sem("ctx_hi"), sem("ctx_split")
        k_made, k_hi, k_lo, k_dup = sem("k_made"), sem("k_hi"), sem("k_lo"), sem("k_dup")
        v_made, v_ready = sem("v_made"), sem("v_ready")
        scores_ready, probs_ready, probs_used = sem("scores_ready"), sem("probs_ready"), sem("probs_used")
        acc_saved = sem("acc_saved")
        block = stack.enter_context(nc.Block())

        LOOPED = (NC - 5) // 2 * 2

        def chunks(engine, one):
            def flags(c):
                return c == 0, c + 1 < NC, c + 2 < NC, c + 3 < NC
            one(0, 0, *flags(0))
            with engine.Fori(0, LOOPED // 2) as i:
                one(i * 2 + 1, 1, False, True, True, True)
                one(i * 2 + 2, 0, False, True, True, True)
            for c in range(LOOPED + 1, NC):
                one(c, c % 2, *flags(c))

        @block.sync
        def _(sp):
            sp.dma_start(x_sb, x[0].rearrange("(a p) n -> p a n", p=P)).then_inc(x_loaded, 16)
            sp.dma_start(wk_raw, wkT).then_inc(wk_loaded, 16)
            sp.dma_start(raw[:], ctxT[0]).then_inc(ctx_loaded, 16)
            sp.dma_start(wq_raw, wqT).then_inc(wq_loaded, 16)
            sp.dma_start(wv_raw, wvT).then_inc(wv_loaded, 16)
            for c in (1, 2):
                sp.wait_ge(ctx_split, c)
                sp.dma_start(raw[:], ctxT[c]).then_inc(ctx_loaded, 16)

            def one(c, par, first, k_next, split_next, load_next):
                if load_next:
                    sp.wait_ge(ctx_split, c + 3)
                    sp.dma_start(raw[:], ctxT[c + 3]).then_inc(ctx_loaded, 16)

            chunks(sp, one)

        @block.gpsimd
        def _(pool):
            nc.gpsimd.memset(ident[:], 0.0).then_inc(const_step, 1)
            nc.gpsimd.memset(zeros[:], 0.0).then_inc(const_ready, 1)
            pool.wait_ge(const_step, 1)
            nc.gpsimd.affine_select(out=ident[:], in_=ident[:], compare_op=ALU.not_equal, fill=1.0,
                                    base=0, pattern=[[-1, P]], channel_multiplier=1).then_inc(const_ready, 1)

        @block.scalar
        def _(act):
            act.wait_ge(sqrt_asked, 1)
            nc.scalar.activation(mv[:, :, 2:3], mv[:, :, 2:3], ACT.Sqrt).then_inc(sqrt_done, 1)

            def k_rows(u, par, g):
                act.wait_ge(k_made, u + 1)
                for j in range(HG):
                    nc.scalar.activation(kst[0:D, par, j, g, :], kp[D * j:D * (j + 1), :],
                                         ACT.Copy).then_inc(k_hi, 1)

            def sigmoid(n, tile, t, g, first):
                act.wait_ge(scores_ready, n + 1)
                if not (first and t < 2):
                    act.wait_ge(probs_used, tile - 1)
                nc.scalar.activation(probs[:, t % 2, g, :], sc[g % 2][:], ACT.Sigmoid).then_inc(probs_ready, 1)

            for g in range(G):
                k_rows(g, 0, g)

            def one(c, par, first, k_next, split_next, load_next):
                for t in range(TC):
                    tile = c * TC + t
                    for g in (0, 1):
                        sigmoid(tile * G + g, tile, t, g, first)
                    if k_next:
                        k_rows(tile + TC, 1 - par, t)
                    for g in (2, 3):
                        sigmoid(tile * G + g, tile, t, g, first)

            chunks(act, one)

        @block.vector
        def _(dve):
            link = Chain(dve, dve_chain)

            def ask_sqrt():
                nc.vector.tensor_copy(mv[:, :, 3:4], mv[:, :, 2:3]).then_inc(sqrt_asked, 1)
                dve.wait_ge(sqrt_done, 1)

            dve.wait_ge(x_loaded, 16)
            layernorm(nc, dve, sqrt_done, x_sb, xn, stats, mv, link, ask_sqrt).then_inc(xn_ready, 1)

            def split(hi, lo, source, done):
                link(nc.vector.tensor_copy(hi, source))
                nc.vector.tensor_tensor(lo, source, f32(hi), ALU.subtract).then_inc(done, 1)

            def split_chunk(c, par):
                dve.wait_ge(ctx_loaded, 16 * c + 16)
                nc.vector.tensor_copy(c_hi[:, par, :, :], raw[:]).then_inc(ctx_hi, 1)
                dve.wait_ge(ctx_hi, c + 1)
                nc.vector.tensor_tensor(c_lo[:, par, :, :], raw[:], f32(c_hi[:, par, :, :]),
                                        ALU.subtract).then_inc(ctx_split, 1)

            def k_rest(u, par, g):
                for j in range(HG):
                    dve.wait_ge(k_hi, u * HG + j + 1)
                    nc.vector.tensor_tensor(kst[D:2 * D, par, j, g, :], kp[D * j:D * (j + 1), :],
                                            f32(kst[0:D, par, j, g, :]), ALU.subtract).then_inc(k_lo, 1)
                nc.vector.tensor_copy(kst[2 * D:3 * D, par, :, g, :],
                                      kst[0:D, par, :, g, :]).then_inc(k_dup, 1)

            def v_out(m, buf, free):
                dve.wait_ge(v_made, m + 1)
                if free:
                    dve.wait_ge(probs_used, m - 1)
                nc.vector.tensor_copy(v[:, buf, :], vp[:]).then_inc(v_ready, 1)

            dve.wait_ge(wk_loaded, 16)
            split(wk_hi[:], wk_lo[:], wk_raw, wk_split)
            split_chunk(0, 0)
            dve.wait_ge(xnT_made, 1)
            nc.vector.tensor_copy(xnT, sc[1][:].rearrange("p (k l) -> p k l", k=KE)).then_inc(xnT_ready, 1)
            dve.wait_ge(wv_loaded, 16)
            split(wv_hi[:], wv_lo[:], wv_raw, wv_split)
            split_chunk(1, 1)
            dve.wait_ge(q_made, 1)
            for j in range(HG):
                link(nc.vector.tensor_scalar_mul(qst[0:D, j, :, :],
                                                 sc[0][D * j:D * (j + 1), :].rearrange("p (g l) -> p g l", g=G),
                                                 float(D) ** -0.5))
                link(nc.vector.scalar_tensor_tensor(
                    out=qst[2 * D:3 * D, j, :, :],
                    in0=sc[0][D * j:D * (j + 1), :].rearrange("p (g l) -> p g l", g=G),
                    scalar=float(D) ** -0.5, in1=f32(qst[0:D, j, :, :]), op0=ALU.mult, op1=ALU.subtract))
            nc.vector.tensor_copy(qst[D:2 * D, :, :, :], qst[0:D, :, :, :]).then_inc(q_ready, 1)
            for g in range(G):
                k_rest(g, 0, g)
            v_out(0, 0, False)

            def one(c, par, first, k_next, split_next, load_next):
                for t in range(TC):
                    tile = c * TC + t
                    if t == TC - 1 and split_next:
                        dve.wait_ge(v_made, tile + 1)
                        split_chunk(c + 2, par)
                    if k_next:
                        k_rest(tile + TC, 1 - par, t)
                    if k_next or t < TC - 1:
                        v_out(tile + 1, (t + 1) % 2, not (first and t == 0))

            chunks(dve, one)
            dve.wait_ge(probs_used, NC * TC)
            nc.vector.tensor_copy(oT[:], acc[:]).then_inc(acc_saved, 1)
            dve.wait_ge(acc_saved, 1)

        @block.tensor
        def _(pe):
            pe.wait_ge(const_ready, 2)
            for b in range(G * L // 512):
                nc.tensor.matmul(acc[:, 2 * b:2 * b + 2, :], zeros[:, 0:P], zeros[:], start=True, stop=True,
                                 skip_group_check=True)
            pe.wait_ge(xn_ready, 1)
            for a in range(LT):
                for k in range(KE):
                    last = nc.tensor.transpose(sc[1][:, k * L + a * P:k * L + (a + 1) * P],
                                               xn[:, a, k * P:(k + 1) * P], ident[:])
            last.then_inc(xnT_made, 1)
            pe.wait_ge(wq_loaded, 16)
            pe.wait_ge(xnT_ready, 1)
            for g in range(G):
                for k in range(KE):
                    last = nc.tensor.matmul(sc[0][:, g * L:(g + 1) * L], wq_raw[:, k, g * P:(g + 1) * P],
                                            xnT[:, k, :], start=k == 0, stop=k == KE - 1)
            last.then_inc(q_made, 1)

            def k_project(u, par, g, free):
                if free:
                    pe.wait_ge(k_lo, u * HG)
                n = 0
                for w, c in ((wk_hi, c_hi), (wk_lo, c_hi), (wk_hi, c_lo)):
                    for k in range(KE):
                        last = nc.tensor.matmul(kp[:], w[:, k, g * P:(g + 1) * P], c[:, par, k, :],
                                                start=n == 0, stop=n == 3 * KE - 1)
                        n += 1
                last.then_inc(k_made, 1)

            def v_project(m, par, t, free):
                if free:
                    pe.wait_ge(v_ready, m)
                n = 0
                for c, w in ((c_hi, wv_hi), (c_hi, wv_lo), (c_lo, wv_hi)):
                    for k in range(KE):
                        last = nc.tensor.matmul(vp[:], c[:, par, k, t * P:(t + 1) * P], w[:, k, :],
                                                start=n == 0, stop=n == 3 * KE - 1)
                        n += 1
                last.then_inc(v_made, 1)

            def scores(n, par, t, g, free):
                if free:
                    pe.wait_ge(probs_ready, n - 1)
                for j in range(HG):
                    last = nc.tensor.matmul(sc[g % 2][:, j * L:(j + 1) * L],
                                            kst[0:3 * D, par, j, g, t * P:(t + 1) * P],
                                            qst[0:3 * D, j, g, :], start=True, stop=True)
                last.then_inc(scores_ready, 1)

            def weigh(tile, t):
                pe.wait_ge(v_ready, tile + 1)
                for g in range(G):
                    pe.wait_ge(probs_ready, tile * G + g + 1)
                    for j in range(HG):
                        h = g * HG + j
                        last = nc.tensor.matmul(acc[D * j:D * (j + 1), g, :], v[:, t % 2, h * D:(h + 1) * D],
                                                probs[:, t % 2, g, j * L:(j + 1) * L], start=False, stop=False,
                                                skip_group_check=True)
                last.then_inc(probs_used, 1)

            pe.wait_ge(wk_split, 1)
            pe.wait_ge(ctx_split, 1)
            for g in range(G):
                k_project(g, 0, g, g > 0)
            pe.wait_ge(wv_split, 1)
            v_project(0, 0, 0, False)
            pe.wait_ge(q_ready, 1)

            def one(c, par, first, k_next, split_next, load_next):
                pe.wait_ge(k_lo, (c + 1) * G * HG)
                pe.wait_ge(k_dup, (c + 1) * G)
                if k_next:
                    pe.wait_ge(ctx_split, c + 2)
                for t in range(TC):
                    tile = c * TC + t
                    for g in (0, 1):
                        scores(tile * G + g, par, t, g, not (first and t == 0))
                    if k_next:
                        k_project(tile + TC, 1 - par, t, True)
                    for g in (2, 3):
                        scores(tile * G + g, par, t, g, True)
                    if k_next or t < TC - 1:
                        ahead = t + 1 if t < TC - 1 else 0
                        v_project(tile + 1, par if ahead else 1 - par, ahead, True)
                    weigh(tile, t)

            chunks(pe, one)


def self_attention(nc, x, woT, wqk, bqk, wv, bv, wn, bn, wo, bo, w12, keep):
    ident, oT, x2, x2nT = keep["ident"], keep["oT"], keep["x2"], keep["x2nT"]
    with ExitStack() as stack:
        def sb(name, shape, dt=F32):
            return stack.enter_context(nc.sbuf_tensor(name, shape, dt))

        def sem(name):
            return stack.enter_context(nc.semaphore(name))

        wqk_sb, wv_sb, wo_sb = sb("wqk_sb", [P, KE, 2 * E]), sb("wvs_sb", [P, KE, E]), sb("wos_sb", [P, KE, E])
        wox_sb = sb("wox_sb", [P, KE, E])
        wn_sb, bqk_sb = sb("wn_sb", [P, KE, H]), sb("bqk_sb", [P, 2 * KE])
        bv_sb, bo_sb, bn_sb = sb("bv_sb", [P, E]), sb("bo_sb", [P, E]), sb("bn_sb", [P, H])
        x_sb, x1, xn, xnT = sb("x_sb", [P, LT, E]), sb("x1", [P, LT, E]), sb("xn1", [P, LT, E]), sb("xn1T", [P, KE, L])
        qkT, vv = sb("qkT", [P, 2 * KE, L]), sb("vv", [P, LT, E])
        ninv = sb("n_inverse", [P, LT, H])
        SW = L + P
        mask, st = sb("mask", [P, SW]), sb("st", [P, H, SW])
        cx, cT = sb("cx", [P, LT, E]), sb("cT", [P, KE, L])
        stats, mv = sb("ln2_stats", [P, LT, 6]), sb("ln2_mv", [P, LT, 4])
        pa = stack.enter_context(nc.psum_tensor("pa", [P, 4, 512], F32))
        pb = stack.enter_context(nc.psum_tensor("pb", [P, 4, 512], F32))

        woT_loaded, x_loaded, wqk_loaded, wv_loaded, rest_loaded, wo_loaded = (
            sem(n) for n in ("woT_ld", "x1_ld", "wqk_ld", "wvs_ld", "rest_ld", "wos_ld"))
        mask_step, mask_ready = sem("mask_step"), sem("mask_ready")
        chain, sqrt_asked, sqrt_done = sem("chain2"), sem("sqrt2_asked"), sem("sqrt2_done")
        pe_done, dve_done, exp_asked, exp_done = sem("pe_done"), sem("dve_done"), sem("exp_asked"), sem("exp_done")
        block = stack.enter_context(nc.Block())

        (PE_OUT1, PE_XNT, PE_QK, PE_V, PE_ST0) = range(1, 6)
        PE_CX = PE_ST0 + G
        PE_CT, PE_OUT2, PE_X2NT = PE_CX + 1, PE_CX + 2, PE_CX + 3
        (DVE_XN, DVE_XNT, DVE_QK, DVE_V, DVE_ST0) = range(1, 6)
        DVE_CX = DVE_ST0 + G
        DVE_CT, DVE_X2N, DVE_X2NT = DVE_CX + 1, DVE_CX + 2, DVE_CX + 3

        @block.sync
        def _(sp):
            sp.dma_start(wox_sb[:], woT).then_inc(woT_loaded, 16)
            sp.dma_start(x_sb[:], x[0].rearrange("(a p) n -> p a n", p=P)).then_inc(x_loaded, 16)
            sp.dma_start(wqk_sb[:], wqk.rearrange("(k p) n -> p k n", p=P)).then_inc(wqk_loaded, 16)
            sp.dma_start(wv_sb[:], wv.rearrange("(k p) n -> p k n", p=P)).then_inc(wv_loaded, 16)
            sp.dma_start(bqk_sb[:], bqk).then_inc(rest_loaded, 16)
            sp.dma_start(wn_sb[:], wn).then_inc(rest_loaded, 16)
            sp.dma_start(bv_sb[:], bv.partition_broadcast(P)).then_inc(rest_loaded, 16)
            sp.dma_start(bn_sb[:], bn.partition_broadcast(P)).then_inc(rest_loaded, 16)
            sp.dma_start(bo_sb[:], bo.partition_broadcast(P)).then_inc(rest_loaded, 16)
            sp.dma_start(wo_sb[:], wo.rearrange("(k p) n -> p k n", p=P)).then_inc(wo_loaded, 16)
            for q in range(RING):
                sp.dma_start(keep["raw"][:, q, :], w12[q]).then_inc(keep["raw_loaded"][q], 16)

        @block.gpsimd
        def _(pool):
            nc.gpsimd.memset(mask[:], 1.0).then_inc(mask_step, 1)
            pool.wait_ge(mask_step, 1)
            for at in (0, L):
                nc.gpsimd.affine_select(out=mask[:, at:at + P], in_=mask[:, at:at + P], compare_op=ALU.is_ge,
                                        fill=0.0, base=0, pattern=[[1, P]],
                                        channel_multiplier=-1).then_inc(mask_ready, 1)

        @block.scalar
        def _(act):
            act.wait_ge(sqrt_asked, 1)
            nc.scalar.activation(mv[:, :, 2:3], mv[:, :, 2:3], ACT.Sqrt).then_inc(sqrt_done, 1)
            act.wait_ge(exp_asked, 1)
            nc.scalar.activation(ninv[:], ninv[:], ACT.Exp, scale=-1.0).then_inc(exp_done, 1)
            act.wait_ge(sqrt_asked, 2)
            nc.scalar.activation(mv[:, :, 2:3], mv[:, :, 2:3], ACT.Sqrt).then_inc(sqrt_done, 1)

        @block.vector
        def _(dve):
            link = Chain(dve, chain)
            asked = [0]

            def ask_sqrt():
                asked[0] += 1
                nc.vector.tensor_copy(mv[:, :, 3:4], mv[:, :, 2:3]).then_inc(sqrt_asked, 1)
                dve.wait_ge(sqrt_done, asked[0])

            dve.wait_ge(x_loaded, 16)
            dve.wait_ge(pe_done, PE_OUT1)
            link(nc.vector.tensor_tensor(x1[:], x_sb[:], pa[:, 0:LT, :], ALU.add))
            layernorm(nc, dve, sqrt_done, x1, xn, stats, mv, link, ask_sqrt).then_inc(dve_done, 1)
            dve.wait_ge(pe_done, PE_XNT)
            nc.vector.tensor_copy(xnT[:].rearrange("p k l -> p (k l)"),
                                  pb[:, 0:2, :].rearrange("p b n -> p (b n)")).then_inc(dve_done, 1)
            dve.wait_ge(rest_loaded, 16 * 5)
            dve.wait_ge(pe_done, PE_QK)
            last = None
            for m in range(2 * KE):
                last = nc.vector.tensor_scalar_add(qkT[:, m, :], pa[:, m // 2, (m % 2) * L:(m % 2 + 1) * L],
                                                   bqk_sb[:, m:m + 1])
            last.then_inc(dve_done, 1)
            dve.wait_ge(pe_done, PE_V)
            for a in range(LT):
                link(nc.vector.tensor_tensor(vv[:, a, :], pb[:, a, :], bv_sb[:], ALU.add))
                link(nc.vector.tensor_tensor(ninv[:, a, :], pb[:, 2, a * H:(a + 1) * H], bn_sb[:], ALU.add))
            nc.vector.tensor_copy(mv[:, 0, 3:4], mv[:, 0, 2:3]).then_inc(exp_asked, 1)
            dve.wait_ge(exp_asked, 1)
            nc.vector.tensor_copy(mv[:, 0, 3:4], mv[:, 0, 2:3]).then_inc(dve_done, 1)
            dve.wait_ge(mask_ready, 2)
            for g in range(G):
                dve.wait_ge(pe_done, PE_ST0 + g)
                ps = pa if g % 2 == 0 else pb
                nc.vector.tensor_tensor(st[:, g * HG:(g + 1) * HG, :], ps[:, 0:HG, 0:SW],
                                        mask[:].unsqueeze(1).to_broadcast([P, HG, SW]), ALU.mult).then_inc(dve_done, 1)
            dve.wait_ge(exp_done, 1)
            dve.wait_ge(pe_done, PE_CX)
            for a in range(LT):
                last = nc.vector.tensor_tensor(cx[:, a, :].rearrange("p (h d) -> p h d", h=H),
                                               pa[:, a, :].rearrange("p (h d) -> p h d", h=H),
                                               ninv[:, a, :].unsqueeze(2).to_broadcast([P, H, D]), ALU.mult)
            last.then_inc(dve_done, 1)
            dve.wait_ge(pe_done, PE_CT)
            nc.vector.tensor_copy(cT[:].rearrange("p k l -> p (k l)"),
                                  pb[:, 0:2, :].rearrange("p b n -> p (b n)")).then_inc(dve_done, 1)
            dve.wait_ge(pe_done, PE_OUT2)
            for a in range(LT):
                link(nc.vector.tensor_tensor(x2[:, a, :], pa[:, a, :], bo_sb[:], ALU.add))
                link(nc.vector.tensor_tensor(x2[:, a, :], x2[:, a, :], x1[:, a, :], ALU.add))
            layernorm(nc, dve, sqrt_done, x2, xn, stats, mv, link, ask_sqrt).then_inc(dve_done, 1)
            dve.wait_ge(pe_done, PE_X2NT)
            nc.vector.tensor_copy(x2nT[:].rearrange("p k l -> p (k l)"),
                                  pb[:, 0:2, :].rearrange("p b n -> p (b n)")).then_inc(dve_done, 1)
            dve.wait_ge(dve_done, DVE_X2NT)

        @block.tensor
        def _(pe):
            def transpose_all(src):
                for a in range(LT):
                    for k in range(KE):
                        at = k * L + a * P
                        last = nc.tensor.transpose(pb[:, at // 512, at % 512:at % 512 + P],
                                                   src[:, a, k * P:(k + 1) * P], ident[:])
                last.then_inc(pe_done, 1)

            def project_rows(srcT, w):
                for a in range(LT):
                    for k in range(KE):
                        last = nc.tensor.matmul(pa[:, a, :], srcT[:, k, a * P:(a + 1) * P], w[:, k, :],
                                                start=k == 0, stop=k == KE - 1)
                last.then_inc(pe_done, 1)

            pe.wait_ge(woT_loaded, 16)
            project_rows(oT, wox_sb)
            pe.wait_ge(dve_done, DVE_XN)
            transpose_all(xn)
            pe.wait_ge(dve_done, DVE_XNT)
            pe.wait_ge(wqk_loaded, 16)
            for m in range(2 * KE):
                for k in range(KE):
                    last = nc.tensor.matmul(pa[:, m // 2, (m % 2) * L:(m % 2 + 1) * L],
                                            wqk_sb[:, k, m * P:(m + 1) * P], xnT[:, k, :],
                                            start=k == 0, stop=k == KE - 1)
            last.then_inc(pe_done, 1)
            pe.wait_ge(wv_loaded, 16)
            pe.wait_ge(rest_loaded, 16 * 5)
            for a in range(LT):
                for k in range(KE):
                    nc.tensor.matmul(pb[:, a, :], xnT[:, k, a * P:(a + 1) * P], wv_sb[:, k, :],
                                     start=k == 0, stop=k == KE - 1)
                for k in range(KE):
                    last = nc.tensor.matmul(pb[:, 2, a * H:(a + 1) * H], xnT[:, k, a * P:(a + 1) * P],
                                            wn_sb[:, k, :], start=k == 0, stop=k == KE - 1)
            last.then_inc(pe_done, 1)
            for g in range(G):
                pe.wait_ge(dve_done, (DVE_QK, DVE_V, DVE_ST0, DVE_ST0 + 1)[g])
                ps = pa if g % 2 == 0 else pb
                for j in range(HG):
                    rows = slice(D * j, D * (j + 1))
                    nc.tensor.matmul(ps[:, j, 0:L], qkT[rows, KE + g, 0:P], qkT[rows, g, :], start=True, stop=True)
                    last = nc.tensor.matmul(ps[:, j, L:SW], qkT[rows, KE + g, P:L], qkT[rows, g, P:L],
                                            start=True, stop=True)
                last.then_inc(pe_done, 1)
            for g in range(G):
                pe.wait_ge(dve_done, max(DVE_ST0 + g, DVE_ST0 + 2))
                for h in range(g * HG, (g + 1) * HG):
                    cols = slice(h * D, (h + 1) * D)
                    nc.tensor.matmul(pa[:, 0, cols], st[:, h, 0:P], vv[:, 0, cols], start=True, stop=True)
                    nc.tensor.matmul(pa[:, 1, cols], st[:, h, P:L], vv[:, 0, cols], start=True, stop=False)
                    last = nc.tensor.matmul(pa[:, 1, cols], st[:, h, L:SW], vv[:, 1, cols], start=False, stop=True)
            last.then_inc(pe_done, 1)
            pe.wait_ge(dve_done, DVE_CX)
            transpose_all(cx)
            pe.wait_ge(dve_done, DVE_CT)
            pe.wait_ge(wo_loaded, 16)
            project_rows(cT, wo_sb)
            pe.wait_ge(dve_done, DVE_X2N)
            transpose_all(xn)


U1 = 2 * HID // (2 * 2 * P)
UH = KH
U3 = KH // 4
RING = 4
AHEAD = 2
FIRST = {1: 0, 2: U1, 3: U1 + UH, 4: U1 + 2 * UH}
TILE0 = {1: 0, 2: KH, 3: 2 * KH}
assert not any(n % RING for n in FIRST.values()) and U3 == RING


def units(engine, one):
    for i in range(U1 // RING):
        for q in range(RING):
            one(1, i, q)
    for layer in (2, 3):
        with engine.Fori(0, UH // RING) as i:
            for q in range(RING):
                one(layer, i, q)
    for q in range(RING):
        one(4, 0, q)


def mlp(nc, w12, wh1, wh2, w3, scales, s3, out, keep):
    x2, x2nT, raw, raw_loaded = keep["x2"], keep["x2nT"], keep["raw"], keep["raw_loaded"]
    with ExitStack() as stack:
        def sb(name, shape, dt=F32):
            return stack.enter_context(nc.sbuf_tensor(name, shape, dt))

        def sem(name):
            return stack.enter_context(nc.semaphore(name))

        w_hi, w_lo = sb("w_hi", [P, RING, UNIT], F32R), sb("w_lo", [P, RING, UNIT], F32R)
        h_hi = [sb(f"h_hi{i}", [P, KH, L], F32R) for i in range(2)]
        h_lo = [sb(f"h_lo{i}", [P, KH, L], F32R) for i in range(2)]
        hf, gate = sb("hf", [P, 2, L]), sb("gate", [P, 2, L])
        scale = sb("scales", [P, 4, KH])
        s3_sb, y = sb("s3_sb", [P, E]), sb("y", [P, LT, E])
        ps = [stack.enter_context(nc.psum_tensor(f"ps{i}", [P, 2, L], F32)) for i in range(4)]
        py = [stack.enter_context(nc.psum_tensor(f"py{i}", [P, E], F32)) for i in range(LT)]

        scales_loaded, stored = sem("scales_ld"), sem("stored")
        w_rounded, w_split = sem("w_rounded"), sem("w_split")
        sums_ready, act_ready, hf_ready = sem("sums_ready"), sem("act_ready"), sem("hf_ready")
        h_rounded, h_ready = sem("h_rounded"), sem("h_ready")
        x_rounded, x_split, y_step, y_ready = sem("x_rounded"), sem("x_split"), sem("y_step"), sem("y_ready")
        block = stack.enter_context(nc.Block())

        @block.sync
        def _(sp):
            for i, s in enumerate(scales):
                sp.dma_start(scale[:, i, :], s).then_inc(scales_loaded, 16)
            sp.dma_start(s3_sb[:], s3.partition_broadcast(P)).then_inc(scales_loaded, 16)

            def one(layer, i, q):
                if layer == 1 and i == 0:
                    return
                source = {1: w12, 2: wh1, 3: wh2, 4: w3}[layer]
                sp.wait_ge(w_split, i * RING + (FIRST[layer] + q - RING + 1))
                sp.dma_start(raw[:, q, :], source[i * RING + q]).then_inc(raw_loaded[q], 16)

            units(sp, one)
            sp.wait_ge(y_ready, 1)
            sp.dma_start(out[0].rearrange("(a p) n -> p a n", p=P), y[:]).then_inc(stored, 16)
            sp.wait_ge(stored, 16)

        @block.scalar
        def _(act):
            act.wait_ge(scales_loaded, 16 * 5)

            def w_round(layer, i, q):
                at = (q + AHEAD) % RING
                act.wait_ge(raw_loaded[at], i * 16 + 16 * (FIRST[layer] // RING + (q + AHEAD) // RING + 1))
                u = i * RING + (FIRST[layer] + q + AHEAD)
                if layer == 1 and u >= RING:
                    act.wait_ge(sums_ready, 2 * (u - RING + 1))
                elif layer > 1:
                    act.wait_ge(sums_ready, u + (U1 - RING + 1))
                nc.scalar.activation(w_hi[:, at, :], raw[:, at, :], ACT.Copy).then_inc(w_rounded, 1)

            for q in range(AHEAD):
                w_round(1, 0, q - AHEAD)

            def one(layer, i, q):
                if not (layer == 4 and q + AHEAD >= U3):
                    w_round(layer, i, q)
                if layer == 1:
                    for n in (2 * (i * RING + q), 2 * (i * RING + q) + 1):
                        act.wait_ge(sums_ready, n + 1)
                        if n >= 2:
                            act.wait_ge(hf_ready, n - 1)
                        nc.scalar.activation(gate[:, n % 2, :], ps[n % 4][:, 0, :], ACT.Silu,
                                             scale=scale[:, 0, n:n + 1]).then_inc(act_ready, 1)
                elif layer < 4:
                    n = i * RING + (TILE0[layer] + q)
                    act.wait_ge(sums_ready, n + 1)
                    act.wait_ge(h_ready, n - 1)
                    nc.scalar.activation(hf[:, q % 2, :], ps[q][:, 0, :], ACT.Gelu,
                                         scale=scale[:, layer, bass.ds(i * RING + q, 1)]).then_inc(act_ready, 1)

            units(act, one)

        @block.vector
        def _(dve):
            nc.vector.tensor_copy(h_hi[1][:, 0:KE, :], x2nT[:]).then_inc(x_rounded, 1)
            dve.wait_ge(x_rounded, 1)
            nc.vector.tensor_tensor(h_lo[1][:, 0:KE, :], x2nT[:], f32(h_hi[1][:, 0:KE, :]),
                                    ALU.subtract).then_inc(x_split, 1)
            dve.wait_ge(scales_loaded, 16 * 5)

            def w_rest(layer, i, q):
                at = (q + AHEAD) % RING
                dve.wait_ge(w_rounded, i * RING + (FIRST[layer] + q + AHEAD + 1))
                nc.vector.tensor_tensor(w_lo[:, at, :], raw[:, at, :], f32(w_hi[:, at, :]),
                                        ALU.subtract).then_inc(w_split, 1)

            def h_split(n, o, slot, to):
                nc.vector.tensor_copy(h_hi[to][:, bass.ds(o, 1), :], hf[:, slot:slot + 1, :]).then_inc(h_rounded, 1)
                dve.wait_ge(h_rounded, n + 1)
                nc.vector.tensor_tensor(h_lo[to][:, bass.ds(o, 1), :], hf[:, slot:slot + 1, :],
                                        f32(h_hi[to][:, bass.ds(o, 1), :]), ALU.subtract).then_inc(h_ready, 1)

            for q in range(AHEAD):
                w_rest(1, 0, q - AHEAD)

            def one(layer, i, q):
                if not (layer == 4 and q + AHEAD >= U3):
                    w_rest(layer, i, q)
                if layer == 1:
                    for n in (2 * (i * RING + q), 2 * (i * RING + q) + 1):
                        dve.wait_ge(act_ready, n + 1)
                        if n >= 2:
                            dve.wait_ge(h_ready, n - 1)
                        nc.vector.scalar_tensor_tensor(out=hf[:, n % 2, :], in0=ps[n % 4][:, 1, :],
                                                       scalar=scale[:, 1, n:n + 1], in1=gate[:, n % 2, :],
                                                       op0=ALU.mult, op1=ALU.mult).then_inc(hf_ready, 1)
                        dve.wait_ge(hf_ready, n + 1)
                        h_split(n, n, n % 2, 0)
                elif layer < 4:
                    n = i * RING + (TILE0[layer] + q)
                    dve.wait_ge(act_ready, n + 1)
                    h_split(n, i * RING + q, q % 2, layer % 2 ^ 1)

            units(dve, one)
            dve.wait_ge(sums_ready, 3 * KH + U3)
            for a in range(LT):
                nc.vector.tensor_tensor(y[:, a, :], py[a][:], s3_sb[:], ALU.mult).then_inc(y_step, 1)
            dve.wait_ge(y_step, LT)
            nc.vector.tensor_tensor(y[:], y[:], x2[:], ALU.add).then_inc(y_ready, 1)

        @block.tensor
        def _(pe):
            pe.wait_ge(x_split, 1)

            def one(layer, i, q):
                pe.wait_ge(w_split, i * RING + (FIRST[layer] + q + 1))
                if layer == 1:
                    hi = w_hi[:, q, :].rearrange("p (w o k n) -> p w o k n", w=2, o=2, k=KE)
                    lo = w_lo[:, q, :].rearrange("p (w o k n) -> p w o k n", w=2, o=2, k=KE)
                    for o in range(2):
                        n = 2 * (i * RING + q) + o
                        if n >= 4:
                            pe.wait_ge(hf_ready, n - 3)
                        for w in range(2):
                            m = 0
                            for wt, x in ((hi, h_hi[1]), (lo, h_hi[1]), (hi, h_lo[1])):
                                for k in range(KE):
                                    last = nc.tensor.matmul(ps[n % 4][:, w, :], wt[:, w, o, k, :], x[:, k, :],
                                                            start=m == 0, stop=m == 3 * KE - 1)
                                    m += 1
                        last.then_inc(sums_ready, 1)
                elif layer < 4:
                    hi = w_hi[:, q, :].rearrange("p (k n) -> p k n", k=KH)
                    lo = w_lo[:, q, :].rearrange("p (k n) -> p k n", k=KH)
                    src = layer % 2
                    pe.wait_ge(h_ready, TILE0[layer])
                    pe.wait_ge(act_ready, i * RING + (TILE0[layer] + q - 3))
                    m = 0
                    for wt, x in ((hi, h_hi[src]), (lo, h_hi[src]), (hi, h_lo[src])):
                        for k in range(KH):
                            last = nc.tensor.matmul(ps[q][:, 0, :], wt[:, k, :], x[:, k, :],
                                                    start=m == 0, stop=m == 3 * KH - 1)
                            m += 1
                    last.then_inc(sums_ready, 1)
                else:
                    hi = w_hi[:, q, :].rearrange("p (k n) -> p k n", k=4)
                    lo = w_lo[:, q, :].rearrange("p (k n) -> p k n", k=4)
                    pe.wait_ge(h_ready, 3 * KH)
                    for a in range(LT):
                        rows = slice(a * P, (a + 1) * P)
                        m = 0
                        for x, wt in ((h_hi[0], hi), (h_hi[0], lo), (h_lo[0], hi)):
                            for k in range(4):
                                last = nc.tensor.matmul(py[a][:], x[:, 4 * q + k, rows], wt[:, k, :],
                                                        start=q == 0 and m == 0, stop=q == U3 - 1 and m == 11)
                                m += 1
                    last.then_inc(sums_ready, 1)

            units(pe, one)


def build(nc, x, ctxT, wqT, wkT, wvT, woT, wqk, bqk, wv, bv, wn, bn, wo, bo,
          w12, wh1, wh2, w3, s1, s2, sh1, sh2, s3, out):
    with ExitStack() as stack:
        def sb(name, shape, dt=F32):
            return stack.enter_context(nc.sbuf_tensor(name, shape, dt))

        keep = {"ident": sb("ident", [P, P]), "zeros": sb("zeros", [P, 512], BF16), "oT": sb("oT", [P, G, L])}
        cross_attention(nc, x, ctxT, wqT, wkT, wvT, keep)
        keep |= {"x2": sb("x2", [P, LT, E]), "x2nT": sb("x2nT", [P, KE, L]), "raw": sb("w_raw", [P, RING, UNIT]),
                 "raw_loaded": [stack.enter_context(nc.semaphore(f"raw_loaded{q}")) for q in range(RING)]}
        self_attention(nc, x, woT, wqk, bqk, wv, bv, wn, bn, wo, bo, w12, keep)
        mlp(nc, w12, wh1, wh2, w3, (s1, s2, sh1, sh2), s3, out, keep)


def kernel(**inputs):
    from concourse import bacc
    from concourse.bass_utils import run_bass_kernel_spmd

    a = {k: np.asarray(v) for k, v in inputs.items()}

    def rows_split(w):
        return w.reshape(-1, P, w.shape[1]).transpose(1, 0, 2)

    def out_tiles(w):
        return w.reshape(w.shape[0] // P, P, w.shape[1] // P, P).transpose(0, 3, 2, 1)

    w1, w2 = (out_tiles(a[f"L0_ffn_{n}_w"]).reshape(U1, 2, P, KE * P).transpose(0, 2, 1, 3) for n in ("w1", "w2"))
    arrays = {
        "x": a["x"],
        "ctxT": a["ctx_1024"][0].reshape(NC, CH, KE, P).transpose(0, 3, 2, 1),
        "wqT": rows_split(a["L0_xattn_Wq"].T),
        "wkT": rows_split(a["L0_xattn_Wk"].T),
        "wvT": rows_split(a["L0_xattn_Wv"].T),
        "woT": rows_split(a["L0_xattn_Wo"].T),
        "wqk": a["L0_attn_Wqk"],
        "bqk": a["L0_attn_bqk"].reshape(2 * KE, P).T,
        "wv": a["L0_attn_Wv"], "bv": a["L0_attn_bv"],
        "wn": rows_split(a["L0_attn_Wn"]), "bn": a["L0_attn_bn"],
        "wo": a["L0_attn_Wo"], "bo": a["L0_attn_bo"],
        "w12": np.stack([w1, w2], axis=2).reshape(U1, P, UNIT),
        "wh1": out_tiles(a["L0_ffn_h1_w"]).reshape(UH, P, UNIT),
        "wh2": out_tiles(a["L0_ffn_h2_w"]).reshape(UH, P, UNIT),
        "w3": a["L0_ffn_w3_w"].T.reshape(U3, 4, P, E).transpose(0, 2, 1, 3).reshape(U3, P, UNIT),
        "s1": a["L0_ffn_w1_s"].reshape(KH, P).T, "s2": a["L0_ffn_w2_s"].reshape(KH, P).T,
        "sh1": a["L0_ffn_h1_s"].reshape(KH, P).T, "sh2": a["L0_ffn_h2_s"].reshape(KH, P).T,
        "s3": a["L0_ffn_w3_s"],
    }
    arrays = {f"{k}_dram": np.ascontiguousarray(v) for k, v in arrays.items()}
    nc = bacc.Bacc("TRN2", target_bir_lowering=False, num_devices=1)
    aps = [nc.dram_tensor(k, v.shape, mybir.dt.from_np(v.dtype), kind="ExternalInput").ap()
           for k, v in arrays.items()]
    out = nc.dram_tensor("out_dram", (1, L, E), F32, kind="ExternalOutput").ap()
    build(nc, *aps, out)
    result = run_bass_kernel_spmd(nc, [arrays], core_ids=[0])
    return result.results[0]["out_dram"]
```

```python
from contextlib import ExitStack

import numpy as np

import concourse.bass as bass
from concourse import mybir

F32 = mybir.dt.float32
F32R = mybir.dt.float32r
BF16 = mybir.dt.bfloat16
ALU = mybir.AluOpType
ACT = mybir.ActivationFunctionType

P = 128
L = 256
E = 512
S = 25088
H = 16
D = E // H
HID = 2048
KE = E // P
KH = HID // P
LT = L // P
HG = P // D
G = H // HG
CH = 512
NC = S // CH
TC = CH // P
EPS = 1e-5
UNIT = KH * P
assert NC * CH == S and G == TC == KE


def f32(ap):
    return ap.bitcast(F32)


def layernorm(nc, dve, x, xn, stats, mv, link, var_ready, sd_ready, times, xn_ready):
    for a in range(LT):
        nc.vector.bn_stats(stats[:, a, :], x[:, a, :])
    link(nc.vector.tensor_copy(mv[:, :, 3:4], x[:, :, 0:1]))
    for a in range(LT):
        link(nc.vector.bn_aggr(mv[:, a, 0:2], stats[:, a, :]))
    nc.vector.tensor_scalar_add(mv[:, :, 2:3], mv[:, :, 1:2], EPS).then_inc(var_ready, 1)
    dve.wait_ge(sd_ready, times)
    link(nc.vector.reciprocal(mv[:, :, 3:4], mv[:, :, 2:3]))
    for a in range(LT):
        nc.vector.tensor_scalar(xn[:, a, :], x[:, a, :], mv[:, a, 0:1], mv[:, a, 3:4],
                                ALU.subtract, ALU.mult).then_inc(xn_ready, 1)


class Chain:

    def __init__(self, engine, sem):
        self.engine, self.sem, self.n = engine, sem, 0

    def __call__(self, instruction):
        self.n += 1
        instruction.then_inc(self.sem, 1)
        self.engine.wait_ge(self.sem, self.n)


def cross_attention(nc, x, ctxT, wqT, wkT, wvT, woT, w_all, keep):
    ident, x1 = keep["ident"], keep["x1"]
    with ExitStack() as stack:
        def sb(name, shape, dt=F32):
            return stack.enter_context(nc.sbuf_tensor(name, shape, dt))

        def sem(name):
            return stack.enter_context(nc.semaphore(name))

        wk_hi, wk_lo = sb("wk_hi", [P, KE, E], F32R), sb("wk_lo", [P, KE, E], F32R)
        wv_hi, wv_lo = sb("wv_hi", [P, KE, E], F32R), sb("wv_lo", [P, KE, E], F32R)
        raw = sb("ctx_raw", [P, KE, CH])
        c_hi, c_lo = sb("c_hi", [P, 2, KE, CH], F32R), sb("c_lo", [P, 2, KE, CH], F32R)
        kst = sb("k_stack", [P, 2, HG, G, CH], F32R)
        qst = sb("q_stack", [P, HG, G, L], F32R)
        v = sb("v", [P, 2, E])
        probs = sb("probs", [P, 2, G, HG * L])
        stats, mv = sb("ln_stats", [P, LT, 6]), sb("ln_mv", [P, LT, 4])
        zeros = sb("zeros", [P, 512], BF16)
        piece, piece_hi = sb("piece", [P, 2, PIECE]), sb("piece_hi", [P, PIECE], F32R)
        rest = sb("rest", [P, PIECE])
        exact, zero, unused = keep["exact"], sb("zero", [P, 1]), sb("unused", [P, 1])
        oT, wo_sb = v[:, :, :].rearrange("p a n -> p (a n)").rearrange("p (g l) -> p g l", g=G), raw
        wk_raw = probs[:, 0, 0:2, :].rearrange("p a b -> p (a b)").rearrange("p (k n) -> p k n", k=KE)
        wv_raw = probs[:, 0, 2:4, :].rearrange("p a b -> p (a b)").rearrange("p (k n) -> p k n", k=KE)
        wq_raw = probs[:, 1, 2:4, :].rearrange("p a b -> p (a b)").rearrange("p (k n) -> p k n", k=KE)
        x_sb = probs[:, 1, 0, :].rearrange("p (a n) -> p a n", a=LT)
        xn = probs[:, 1, 1, :].rearrange("p (a n) -> p a n", a=LT)
        xnT = v[:, :, :].rearrange("p a n -> p (a n)").rearrange("p (k l) -> p k l", k=KE)

        sc = [stack.enter_context(nc.psum_tensor(f"sc{i}", [P, HG * L], F32)) for i in range(2)]
        kp = stack.enter_context(nc.psum_tensor("kp", [P, CH], F32))
        vp = stack.enter_context(nc.psum_tensor("vp", [P, E], F32))
        acc = stack.enter_context(nc.psum_tensor("acc", [P, G, L], F32))

        x_loaded, wq_loaded, wo_loaded = sem("x_loaded"), sem("wq_loaded"), sem("wox_loaded")
        wk_loaded, wv_loaded, ctx_loaded = sem("wk_loaded"), sem("wv_loaded"), sem("ctx_loaded")
        ident_zero, const_ready, chain = sem("ident_zero"), sem("const_ready"), sem("dve_chain")
        var_ready, sd_ready, xn_ready = sem("var_ready"), sem("sd_ready"), sem("xn_ready")
        xnT_made, xnT_ready, q_made = sem("xnT_made"), sem("xnT_ready"), sem("q_made")
        q_hi, q_lo, q_dup = sem("q_hi"), sem("q_lo"), sem("q_dup")
        wk_hi_done, wv_hi_done = sem("wk_hi_done"), sem("wv_hi_done")
        wk_split, wv_split = sem("wk_split"), sem("wv_split")
        ctx_hi, ctx_split = sem("ctx_hi"), sem("ctx_split")
        k_made, k_hi, k_lo, k_dup = sem("k_made"), sem("k_hi"), sem("k_lo"), sem("k_dup")
        v_made, v_ready = sem("v_made"), sem("v_ready")
        scores_ready, probs_ready, probs_used = sem("scores_ready"), sem("probs_ready"), sem("probs_used")
        piece_loaded = [sem(f"piece_loaded{i}") for i in range(2)]
        scan_ready, piece_rounded, piece_used = sem("scan_ready"), sem("piece_rounded"), sem("piece_used")
        rest_compared, exact_counted = sem("rest_compared"), sem("exact_counted")
        o_saved, o_projected, x1_ready = sem("o_saved"), sem("o_projected"), sem("x1_ready")
        block = stack.enter_context(nc.Block())
        x_rows = x[0].rearrange("(a p) n -> p a n", p=P)
        SCALE = float(D) ** -0.5

        def q_of(j):
            return sc[0][D * j:D * (j + 1), :].rearrange("p (g l) -> p g l", g=G)

        k_first = (kp[:], vp[:], sc[1][:, 0:CH], sc[1][:, CH:2 * CH])

        LOOPED = (NC - 5) // 2 * 2
        assert LOOPED == UNITS and UNIT == TC * PIECE

        def chunks(engine, one):
            def flags(c):
                return c == 0, c + 1 < NC, c + 2 < NC, c + 3 < NC, False
            one(0, 0, *flags(0))
            with engine.Fori(0, LOOPED // 2) as i:
                one(i * 2 + 1, 1, False, True, True, True, True)
                one(i * 2 + 2, 0, False, True, True, True, True)
            for c in range(LOOPED + 1, NC):
                one(c, c % 2, *flags(c))

        @block.sync
        def _(sp):
            sp.dma_start(x_sb, x_rows).then_inc(x_loaded, 16)
            sp.dma_start(wk_raw, wkT).then_inc(wk_loaded, 16)
            sp.dma_start(wq_raw, wqT).then_inc(wq_loaded, 16)
            sp.dma_start(raw[:], ctxT[0]).then_inc(ctx_loaded, 16)
            sp.dma_start(wv_raw, wvT).then_inc(wv_loaded, 16)
            for c in (1, 2):
                sp.wait_ge(ctx_split, c)
                sp.dma_start(raw[:], ctxT[c]).then_inc(ctx_loaded, 16)
            sp.dma_start(x1[:], x_rows).then_inc(x_loaded, 16)
            for n in range(2):
                sp.dma_start(piece[:, n, :], w_all[0][:, n * PIECE:(n + 1) * PIECE]).then_inc(piece_loaded[n], 16)

            def one(c, par, first, k_next, split_next, load_next, looped):
                if load_next:
                    sp.wait_ge(ctx_split, c + 3)
                    sp.dma_start(raw[:], ctxT[c + 3]).then_inc(ctx_loaded, 16)
                if looped:
                    for n in range(2, TC + 2):
                        u = c - 1 if n < TC else c % UNITS
                        sp.wait_ge(piece_used, c * TC + (n - 2 - TC + 1))
                        sp.dma_start(piece[:, n % 2, :], w_all[u][:, n % TC * PIECE:(n % TC + 1) * PIECE]
                                     ).then_inc(piece_loaded[n % 2], 16)

            chunks(sp, one)
            sp.wait_ge(ctx_split, NC)
            sp.dma_start(wo_sb[:], woT).then_inc(wo_loaded, 16)

        @block.gpsimd
        def _(pool):
            nc.gpsimd.memset(ident[:], 0.0).then_inc(ident_zero, 1)
            nc.gpsimd.memset(zeros[:], 0.0).then_inc(const_ready, 1)
            pool.wait_ge(ident_zero, 1)
            nc.gpsimd.affine_select(out=ident[:], in_=ident[:], compare_op=ALU.not_equal, fill=1.0,
                                    base=0, pattern=[[-1, P]], channel_multiplier=1).then_inc(const_ready, 1)
            pool.wait_ge(wv_hi_done, 1)
            nc.gpsimd.tensor_tensor(wv_lo[:], wv_raw, f32(wv_hi[:]), ALU.subtract).then_inc(wv_split, 1)
            pool.wait_ge(wv_split, 1)
            for j in range(HG):
                pool.wait_ge(q_hi, j + 1)
                if j:
                    pool.wait_ge(q_dup, j)
                nc.gpsimd.tensor_copy(qst[D:2 * D, j, :, :], qst[0:D, j, :, :]).then_inc(q_dup, 1)
            pool.wait_ge(q_dup, HG)
            pool.wait_ge(ctx_hi, 2)
            nc.gpsimd.tensor_tensor(c_lo[:, 1, :, :], raw[:], f32(c_hi[:, 1, :, :]), ALU.subtract).then_inc(ctx_split, 1)
            pool.wait_ge(ctx_split, 2)
            nc.gpsimd.memset(exact[:], 0.0).then_inc(scan_ready, 1)
            nc.gpsimd.memset(zero[:], 0.0).then_inc(scan_ready, 1)
            pool.wait_ge(scan_ready, 2)

            with pool.Fori(0, UNITS) as u:
                for t in range(TC):
                    n = u * TC + t
                    pool.wait_ge(piece_loaded[t % 2], u * (TC // 2 * 16) + (t // 2 + 1) * 16)
                    nc.gpsimd.tensor_tensor(piece_hi[:], piece[:, t % 2, :], zero[:].to_broadcast([P, PIECE]), ALU.add
                                            ).then_inc(piece_rounded, 1)
                    pool.wait_ge(piece_rounded, n + 1)
                    nc.gpsimd.tensor_tensor(rest[:], piece[:, t % 2, :], f32(piece_hi[:]),
                                            ALU.subtract).then_inc(piece_used, 1)
                    pool.wait_ge(piece_used, n + 1)
                    nc.gpsimd.tensor_tensor(unused[:], zero[:], zero[:], ALU.add)
                    nc.gpsimd.tensor_scalar(rest[:], rest[:], 0.0, None, ALU.is_equal).then_inc(rest_compared, 1)
                    pool.wait_ge(rest_compared, n + 1)
                    nc.gpsimd.tensor_tensor(exact[:], exact[:], rest[:], ALU.add).then_inc(exact_counted, 1)
                    pool.wait_ge(exact_counted, n + 1)

        @block.scalar
        def _(act):
            act.wait_ge(var_ready, 1)
            nc.scalar.activation(mv[:, :, 2:3], mv[:, :, 2:3], ACT.Sqrt).then_inc(sd_ready, 1)

            def k_rows(u, par, g, source):
                act.wait_ge(k_made, u + 1)
                for j in range(HG):
                    nc.scalar.activation(kst[0:D, par, j, g, :], source[D * j:D * (j + 1), :],
                                         ACT.Copy).then_inc(k_hi, 1)

            def sigmoid(n, tile, t, g, first):
                act.wait_ge(scores_ready, n + 1)
                if not (first and t < 2):
                    act.wait_ge(probs_used, tile - 1)
                nc.scalar.activation(probs[:, t % 2, g, :], sc[g % 2][:], ACT.Sigmoid).then_inc(probs_ready, 1)

            def rounded(hi, source, loaded, count, done):
                act.wait_ge(loaded, count)
                nc.scalar.activation(hi, source, ACT.Copy).then_inc(done, 1)

            rounded(wk_hi[:], wk_raw, wk_loaded, 16, wk_hi_done)
            rounded(c_hi[:, 0, :, :], raw[:], ctx_loaded, 16, ctx_hi)
            rounded(wv_hi[:], wv_raw, wv_loaded, 16, wv_hi_done)
            act.wait_ge(q_made, 1)
            for j in range(HG):
                nc.scalar.activation(qst[0:D, j, :, :], q_of(j), ACT.Copy, scale=SCALE).then_inc(q_hi, 1)
            for g in range(G):
                k_rows(g, 0, g, k_first[g])
                if g == 1:
                    rounded(c_hi[:, 1, :, :], raw[:], ctx_loaded, 32, ctx_hi)

            def one(c, par, first, k_next, split_next, load_next, looped):
                for t in range(TC):
                    tile = c * TC + t
                    for g in (0, 1):
                        sigmoid(tile * G + g, tile, t, g, first)
                    if k_next:
                        k_rows(tile + TC, 1 - par, t, kp[:])
                    for g in (2, 3):
                        sigmoid(tile * G + g, tile, t, g, first)

            chunks(act, one)

        @block.vector
        def _(dve):
            link = Chain(dve, chain)
            dve.wait_ge(x_loaded, 16)
            layernorm(nc, dve, x_sb, xn, stats, mv, link, var_ready, sd_ready, 1, xn_ready)

            def split_chunk(c, par):
                dve.wait_ge(ctx_loaded, 16 * c + 16)
                nc.vector.tensor_copy(c_hi[:, par, :, :], raw[:]).then_inc(ctx_hi, 1)
                dve.wait_ge(ctx_hi, c + 1)
                nc.vector.tensor_tensor(c_lo[:, par, :, :], raw[:], f32(c_hi[:, par, :, :]),
                                        ALU.subtract).then_inc(ctx_split, 1)

            def k_rest(u, par, g, source):
                for j in range(HG):
                    dve.wait_ge(k_hi, u * HG + j + 1)
                    nc.vector.tensor_tensor(kst[D:2 * D, par, j, g, :], source[D * j:D * (j + 1), :],
                                            f32(kst[0:D, par, j, g, :]), ALU.subtract).then_inc(k_lo, 1)
                nc.vector.tensor_copy(kst[2 * D:3 * D, par, :, g, :],
                                      kst[0:D, par, :, g, :]).then_inc(k_dup, 1)

            def v_out(m, buf, free):
                dve.wait_ge(v_made, m + 1)
                if free:
                    dve.wait_ge(probs_used, m - 1)
                nc.vector.tensor_copy(v[:, buf, :], vp[:]).then_inc(v_ready, 1)

            dve.wait_ge(xnT_made, 1)
            nc.vector.tensor_copy(xnT, sc[1][:].rearrange("p (k l) -> p k l", k=KE)).then_inc(xnT_ready, 1)
            dve.wait_ge(wk_hi_done, 1)
            nc.vector.tensor_tensor(wk_lo[:], wk_raw, f32(wk_hi[:]), ALU.subtract).then_inc(wk_split, 1)
            dve.wait_ge(ctx_hi, 1)
            nc.vector.tensor_tensor(c_lo[:, 0, :, :], raw[:], f32(c_hi[:, 0, :, :]), ALU.subtract).then_inc(ctx_split, 1)
            for j in range(HG):
                dve.wait_ge(q_hi, j + 1)
                nc.vector.scalar_tensor_tensor(out=qst[2 * D:3 * D, j, :, :], in0=q_of(j), scalar=SCALE,
                                               in1=f32(qst[0:D, j, :, :]), op0=ALU.mult,
                                               op1=ALU.subtract).then_inc(q_lo, 1)
            for g in range(G):
                k_rest(g, 0, g, k_first[g])
            v_out(0, 0, False)

            def one(c, par, first, k_next, split_next, load_next, looped):
                for t in range(TC):
                    tile = c * TC + t
                    if t == TC - 1 and split_next:
                        dve.wait_ge(v_made, tile + 1)
                        split_chunk(c + 2, par)
                    if k_next:
                        k_rest(tile + TC, 1 - par, t, kp[:])
                    if k_next or t < TC - 1:
                        v_out(tile + 1, (t + 1) % 2, not (first and t == 0))

            chunks(dve, one)
            dve.wait_ge(probs_used, NC * TC)
            for g in range(G):
                nc.vector.tensor_copy(oT[:, g, :], acc[:, g, :]).then_inc(o_saved, 1)
            dve.wait_ge(x_loaded, 32)
            for a, projected in enumerate((kp, vp)):
                dve.wait_ge(o_projected, a + 1)
                nc.vector.tensor_tensor(x1[:, a, :], x1[:, a, :], projected[:], ALU.add).then_inc(x1_ready, 1)
            dve.wait_ge(x1_ready, LT)

        @block.tensor
        def _(pe):
            pe.wait_ge(const_ready, 2)
            for b in range(G * L // 512):
                nc.tensor.matmul(acc[:, 2 * b:2 * b + 2, :], zeros[:, 0:P], zeros[:], start=True, stop=True,
                                 skip_group_check=True)
            for a in range(LT):
                pe.wait_ge(xn_ready, a + 1)
                for k in range(KE):
                    last = nc.tensor.transpose(sc[1][:, k * L + a * P:k * L + (a + 1) * P],
                                               xn[:, a, k * P:(k + 1) * P], ident[:])
            last.then_inc(xnT_made, 1)
            pe.wait_ge(wq_loaded, 16)
            pe.wait_ge(xnT_ready, 1)
            for g in range(G):
                for k in range(KE):
                    last = nc.tensor.matmul(sc[0][:, g * L:(g + 1) * L], wq_raw[:, k, g * P:(g + 1) * P],
                                            xnT[:, k, :], start=k == 0, stop=k == KE - 1)
            last.then_inc(q_made, 1)

            def k_project(u, par, g, to, free):
                if free:
                    pe.wait_ge(k_lo, u * HG)
                n = 0
                for w, c in ((wk_hi, c_hi), (wk_lo, c_hi), (wk_hi, c_lo)):
                    for k in range(KE):
                        last = nc.tensor.matmul(to, w[:, k, g * P:(g + 1) * P], c[:, par, k, :],
                                                start=n == 0, stop=n == 3 * KE - 1)
                        n += 1
                last.then_inc(k_made, 1)

            def v_project(m, par, t, free):
                if free:
                    pe.wait_ge(v_ready, m)
                n = 0
                for c, w in ((c_hi, wv_hi), (c_hi, wv_lo), (c_lo, wv_hi)):
                    for k in range(KE):
                        last = nc.tensor.matmul(vp[:], c[:, par, k, t * P:(t + 1) * P], w[:, k, :],
                                                start=n == 0, stop=n == 3 * KE - 1)
                        n += 1
                last.then_inc(v_made, 1)

            def scores(n, par, t, g, free):
                if free:
                    pe.wait_ge(probs_ready, n - 1)
                for j in range(HG):
                    last = nc.tensor.matmul(sc[g % 2][:, j * L:(j + 1) * L],
                                            kst[0:3 * D, par, j, g, t * P:(t + 1) * P],
                                            qst[0:3 * D, j, g, :], start=True, stop=True)
                last.then_inc(scores_ready, 1)

            def weigh(tile, t):
                pe.wait_ge(v_ready, tile + 1)
                for g in range(G):
                    pe.wait_ge(probs_ready, tile * G + g + 1)
                    for j in range(HG):
                        h = g * HG + j
                        last = nc.tensor.matmul(acc[D * j:D * (j + 1), g, :], v[:, t % 2, h * D:(h + 1) * D],
                                                probs[:, t % 2, g, j * L:(j + 1) * L], start=False, stop=False,
                                                skip_group_check=True)
                last.then_inc(probs_used, 1)

            pe.wait_ge(wk_split, 1)
            pe.wait_ge(ctx_split, 1)
            for g in range(G):
                k_project(g, 0, g, k_first[g], False)
            pe.wait_ge(wv_split, 1)
            pe.wait_ge(k_lo, 2 * HG)
            v_project(0, 0, 0, False)
            pe.wait_ge(q_lo, HG)
            pe.wait_ge(q_dup, HG)

            def one(c, par, first, k_next, split_next, load_next, looped):
                pe.wait_ge(k_lo, (c + 1) * G * HG)
                pe.wait_ge(k_dup, (c + 1) * G)
                if k_next:
                    pe.wait_ge(ctx_split, c + 2)
                for t in range(TC):
                    tile = c * TC + t
                    for g in (0, 1):
                        scores(tile * G + g, par, t, g, not (first and t == 0))
                    if k_next:
                        k_project(tile + TC, 1 - par, t, kp[:], True)
                    elif t < TC - 1:
                        v_project(tile + 1, par, t + 1, True)
                    for g in (2, 3):
                        scores(tile * G + g, par, t, g, True)
                    if k_next:
                        ahead = t + 1 if t < TC - 1 else 0
                        v_project(tile + 1, par if ahead else 1 - par, ahead, True)
                    weigh(tile, t)

            chunks(pe, one)
            pe.wait_ge(wo_loaded, 16)
            for a, to in enumerate((kp, vp)):
                for g in range(G):
                    pe.wait_ge(o_saved, g + 1)
                    last = nc.tensor.matmul(to[:], oT[:, g, a * P:(a + 1) * P], wo_sb[:, g, :],
                                            start=g == 0, stop=g == G - 1)
                last.then_inc(o_projected, 1)


def self_attention(nc, wqk, bqk, wv, bv, wn, bn, wo, bo, w_all, keep):
    ident, x1, x2, xT_psum = keep["ident"], keep["x1"], keep["x2"], keep["xT_psum"]
    raw, raw_loaded, w_hi, w_lo = keep["raw"], keep["raw_loaded"], keep["w_hi"], keep["w_lo"]
    w_rounded, w_split = keep["w_rounded"], keep["w_split"]
    SW = L + P
    with ExitStack() as stack:
        def sb(name, shape, dt=F32):
            return stack.enter_context(nc.sbuf_tensor(name, shape, dt))

        def sem(name):
            return stack.enter_context(nc.semaphore(name))

        wqk_sb, wv_sb, wo_sb = sb("wqk_sb", [P, KE, 2 * E]), sb("wvs_sb", [P, KE, E]), sb("wos_sb", [P, KE, E])
        wn_sb, bqk_sb = sb("wn_sb", [P, KE, H]), sb("bqk_sb", [P, 2 * KE])
        bv_sb, bo_sb, bn_sb, bn_neg = sb("bv_sb", [P, E]), sb("bo_sb", [P, E]), sb("bn_sb", [H, 1]), sb("bn_neg", [H, 1])
        xn, xnT = sb("xn1", [P, LT, E]), sb("xn1T", [P, KE, L])
        qT, kT, v = sb("qT", [P, G, L]), sb("kT", [P, G, L]), sb("vs", [P, LT, E])
        n_inv, heads, n_rows = sb("n_inv", [H, L]), sb("heads", [H, G, P]), sb("n_rows", [P, G, L])
        ones, inexact, differs = sb("ones", [P, 1]), sb("inexact", [P, 1]), sb("differs", [P, PIECE])
        mask, st, cT = sb("mask", [P, SW]), sb("st", [P, H, SW]), sb("cT", [P, G, L])
        stats, mv = sb("ln2_stats", [P, LT, 6]), sb("ln2_mv", [P, LT, 4])
        qk_p = [stack.enter_context(nc.psum_tensor(f"qk_p{i}", [P, 2, L], F32)) for i in range(2)]
        st_p = stack.enter_context(nc.psum_tensor("st_p", [P, HG, 512], F32))
        cx_p = xT_psum[:, :, :].rearrange("p a n -> p (a n)").rearrange("p (g l) -> p g l", g=G)
        v_p, rows_p = st_p[:, 0:LT, :], st_p[:, LT:2 * LT, :].rearrange("p b n -> p (b n)").rearrange("p (g l) -> p g l", g=G)
        n_p = qk_p[1][0:H, 0, :]

        wqk_loaded, wv_loaded, bias_loaded, wo_loaded = (
            sem(n) for n in ("wqk_ld", "wvs_ld", "bias_ld", "wos_ld"))
        mask_one, heads_one, heads_step, const_ready = (
            sem("mask_one"), sem("heads_one"), sem("heads_step"), sem("const2_ready"))
        chain, var_ready, sd_ready, xn_ready = sem("chain2"), sem("var2"), sem("sd2"), sem("xn2_ready")
        xT_made, xT_ready, v_made, v_ready = sem("xT_made"), sem("xT_ready"), sem("vs_made"), sem("vs_ready")
        n_made, bn_ready, n_ready, rows_made, rows_ready = (
            sem("n_made"), sem("bn_ready"), sem("n_ready"), sem("rows_made"), sem("rows_ready"))
        qk_made, q_ready, k_ready = sem("qk_made"), sem("qs_ready"), sem("ks_ready")
        st_made, st_ready, cx_made, cx_ready = sem("st_made"), sem("st_ready"), sem("cx_made"), sem("cx_ready")
        differs_ready, inexact_ready = sem("differs_ready"), sem("inexact_ready")
        ones_ready, inexact_made = sem("ones_ready"), sem("inexact_made")
        x1b_ready, out_made, x2_ready = sem("x1b_ready"), sem("out_made"), sem("x2_ready")
        block = stack.enter_context(nc.Block())

        @block.sync
        def _(sp):
            sp.dma_start(wv_sb[:], wv).then_inc(wv_loaded, 16)
            sp.dma_start(wn_sb[:], wn).then_inc(bias_loaded, 16)
            sp.dma_start(bqk_sb[:], bqk).then_inc(bias_loaded, 16)
            sp.dma_start(bn_sb[:], bn).then_inc(bias_loaded, 16)
            sp.dma_start(bv_sb[:], bv.partition_broadcast(P)).then_inc(bias_loaded, 16)
            sp.dma_start(bo_sb[:], bo.partition_broadcast(P)).then_inc(bias_loaded, 16)
            sp.dma_start(wqk_sb[:], wqk).then_inc(wqk_loaded, 16)
            sp.dma_start(wo_sb[:], wo).then_inc(wo_loaded, 16)
            for q in range(RING):
                sp.dma_start(raw[:, q, :], w_all[q]).then_inc(raw_loaded[q], 16)

        @block.gpsimd
        def _(pool):
            nc.gpsimd.memset(ones[:], 1.0).then_inc(ones_ready, 1)
            nc.gpsimd.memset(heads[:], 1.0).then_inc(heads_one, 1)
            nc.gpsimd.memset(mask[:], 1.0).then_inc(mask_one, 1)
            pool.wait_ge(heads_one, 1)
            nc.gpsimd.affine_select(out=heads[:], in_=heads[:], compare_op=ALU.is_ge, fill=0.0, base=0,
                                    pattern=[[P, G], [1, P]], channel_multiplier=-D).then_inc(heads_step, 1)
            pool.wait_ge(heads_step, 1)
            nc.gpsimd.affine_select(out=heads[:], in_=heads[:], compare_op=ALU.is_ge, fill=0.0, base=D - 1,
                                    pattern=[[-P, G], [-1, P]], channel_multiplier=D).then_inc(const_ready, 1)
            pool.wait_ge(mask_one, 1)
            for at in (0, L):
                nc.gpsimd.affine_select(out=mask[:, at:at + P], in_=mask[:, at:at + P], compare_op=ALU.is_ge,
                                        fill=0.0, base=0, pattern=[[1, P]],
                                        channel_multiplier=-1).then_inc(const_ready, 1)

        @block.scalar
        def _(act):
            act.wait_ge(var_ready, 1)
            nc.scalar.activation(mv[:, :, 2:3], mv[:, :, 2:3], ACT.Sqrt).then_inc(sd_ready, 1)
            act.wait_ge(bn_ready, 1)
            act.wait_ge(n_made, 1)
            nc.scalar.activation(n_inv[:], n_p, ACT.Exp, bias=bn_neg[:], scale=-1.0).then_inc(n_ready, 1)
            act.wait_ge(bias_loaded, 16 * 5)
            for g in range(G):
                act.wait_ge(qk_made, g + 1)
                nc.scalar.activation(qT[:, g, :], qk_p[g % 2][:, 0, :], ACT.Identity,
                                     bias=bqk_sb[:, g:g + 1]).then_inc(q_ready, 1)
            for q in range(AHEAD):
                act.wait_ge(raw_loaded[q], 16)
                nc.scalar.activation(w_hi[:, q, :], raw[:, q, :], ACT.Copy).then_inc(w_rounded, 1)
            act.wait_ge(var_ready, 2)
            nc.scalar.activation(mv[:, :, 2:3], mv[:, :, 2:3], ACT.Sqrt).then_inc(sd_ready, 1)

        @block.vector
        def _(dve):
            link = Chain(dve, chain)
            layernorm(nc, dve, x1, xn, stats, mv, link, var_ready, sd_ready, 1, xn_ready)
            dve.wait_ge(bias_loaded, 16 * 5)
            nc.vector.tensor_scalar_mul(bn_neg[:], bn_sb[:], -1.0).then_inc(bn_ready, 1)
            for a in range(LT):
                dve.wait_ge(xT_made, a + 1)
                nc.vector.tensor_copy(xnT[:, :, a * P:(a + 1) * P],
                                      xT_psum[:, a, :].rearrange("p (k l) -> p k l", k=KE)).then_inc(xT_ready, 1)
            for a in range(LT):
                nc.vector.tensor_tensor(x1[:, a, :], x1[:, a, :], bo_sb[:], ALU.add).then_inc(x1b_ready, 1)
            for a in range(LT):
                dve.wait_ge(v_made, a + 1)
                nc.vector.tensor_tensor(v[:, a, :], v_p[:, a, :], bv_sb[:], ALU.add).then_inc(v_ready, 1)

            def keys(g):
                dve.wait_ge(q_ready, g + 1)
                nc.vector.tensor_scalar_add(kT[:, g, :], qk_p[g % 2][:, 1, :],
                                            bqk_sb[:, KE + g:KE + g + 1]).then_inc(k_ready, 1)

            def masked(g):
                dve.wait_ge(st_made, g + 1)
                nc.vector.tensor_tensor(st[:, g * HG:(g + 1) * HG, :], st_p[:, :, 0:SW],
                                        mask[:].unsqueeze(1).to_broadcast([P, HG, SW]), ALU.mult).then_inc(st_ready, 1)

            def weighed(g):
                dve.wait_ge(cx_made, g + 1)
                nc.vector.tensor_tensor(cT[:, g, :], cx_p[:, g, :], n_rows[:, g, :], ALU.mult).then_inc(cx_ready, 1)

            def w_rest(q):
                dve.wait_ge(w_rounded, q + 1)
                nc.vector.tensor_tensor(w_lo[:, q, :], raw[:, q, :], f32(w_hi[:, q, :]),
                                        ALU.subtract).then_inc(w_split, 1)

            keys(0)
            dve.wait_ge(rows_made, 1)
            nc.vector.tensor_copy(n_rows[:], rows_p).then_inc(rows_ready, 1)
            dve.wait_ge(rows_ready, 1)
            keys(1)
            dve.wait_ge(const_ready, 3)
            masked(0)
            keys(2)
            nc.vector.tensor_scalar(differs[:], keep["exact"][:], float(PIECES), None,
                                    ALU.not_equal).then_inc(differs_ready, 1)
            dve.wait_ge(differs_ready, 1)
            nc.vector.tensor_reduce(inexact[:], differs[:], mybir.AxisListType.X, ALU.max).then_inc(inexact_ready, 1)
            masked(1)
            keys(3)
            masked(2)
            w_rest(0)
            masked(3)
            w_rest(1)
            dve.wait_ge(cx_made, 2)
            weighed(0)
            weighed(1)
            dve.wait_ge(cx_made, G)
            weighed(2)
            weighed(3)
            dve.wait_ge(x1b_ready, LT)
            for a in range(LT):
                dve.wait_ge(out_made, a + 1)
                nc.vector.tensor_tensor(x2[:, a, :], qk_p[a][:].rearrange("p b n -> p (b n)"), x1[:, a, :],
                                        ALU.add).then_inc(x2_ready, 1)
            dve.wait_ge(inexact_made, 1)
            nc.vector.tensor_copy(keep["any_inexact"][:], st_p[0:1, 0, 0:1]).then_inc(keep["inexact_ready"], 1)
            dve.wait_ge(x2_ready, LT)
            layernorm(nc, dve, x2, xn, stats, mv, link, var_ready, sd_ready, 2, xn_ready)

        @block.tensor
        def _(pe):
            def transposed(done):
                for a in range(LT):
                    pe.wait_ge(xn_ready, done + a + 1)
                    for k in range(KE):
                        last = nc.tensor.transpose(xT_psum[:, a, k * P:(k + 1) * P],
                                                   xn[:, a, k * P:(k + 1) * P], ident[:])
                    last.then_inc(xT_made, 1)

            transposed(0)
            pe.wait_ge(wv_loaded, 16)
            for a in range(LT):
                pe.wait_ge(xT_ready, a + 1)
                for k in range(KE):
                    last = nc.tensor.matmul(v_p[:, a, :], xnT[:, k, a * P:(a + 1) * P], wv_sb[:, k, :],
                                            start=k == 0, stop=k == KE - 1)
                last.then_inc(v_made, 1)
            pe.wait_ge(bias_loaded, 16 * 5)
            for k in range(KE):
                last = nc.tensor.matmul(n_p, wn_sb[:, k, :], xnT[:, k, :], start=k == 0, stop=k == KE - 1)
            last.then_inc(n_made, 1)
            pe.wait_ge(wqk_loaded, 16)

            def queries_keys(g):
                if g == 1:
                    pe.wait_ge(n_ready, 1)
                elif g > 1:
                    pe.wait_ge(q_ready, g - 1)
                    pe.wait_ge(k_ready, g - 1)
                for b in range(2):
                    for k in range(KE):
                        last = nc.tensor.matmul(qk_p[g % 2][:, b, :], wqk_sb[:, k, b * E + g * P:b * E + (g + 1) * P],
                                                xnT[:, k, :], start=k == 0, stop=k == KE - 1)
                last.then_inc(qk_made, 1)

            def scores(g):
                pe.wait_ge(q_ready, g + 1)
                pe.wait_ge(k_ready, g + 1)
                if g:
                    pe.wait_ge(st_ready, g)
                else:
                    pe.wait_ge(v_ready, LT)
                    pe.wait_ge(rows_ready, 1)
                for j in range(HG):
                    rows = slice(D * j, D * (j + 1))
                    nc.tensor.matmul(st_p[:, j, 0:L], kT[rows, g, 0:P], qT[rows, g, :], start=True, stop=True)
                    last = nc.tensor.matmul(st_p[:, j, L:SW], kT[rows, g, P:L], qT[rows, g, P:L],
                                            start=True, stop=True)
                last.then_inc(st_made, 1)

            def weigh(g):
                pe.wait_ge(st_ready, g + 1)
                for s in range(LT):
                    for j in range(HG):
                        h = g * HG + j
                        last = nc.tensor.matmul(cx_p[D * j:D * (j + 1), g, s * P:L], v[:, s, h * D:(h + 1) * D],
                                                st[:, h, s * L:s * L + L - s * P], start=s == 0, stop=s == LT - 1)
                last.then_inc(cx_made, 1)

            queries_keys(0)
            pe.wait_ge(n_ready, 1)
            pe.wait_ge(const_ready, 1)
            for g in range(G):
                last = nc.tensor.matmul(rows_p[:, g, :], heads[:, g, :], n_inv[:], start=True, stop=True)
            last.then_inc(rows_made, 1)
            queries_keys(1)
            scores(0)
            queries_keys(2)
            scores(1)
            weigh(0)
            queries_keys(3)
            scores(2)
            weigh(1)
            scores(3)
            weigh(2)
            weigh(3)
            pe.wait_ge(ones_ready, 1)
            pe.wait_ge(inexact_ready, 1)
            pe.wait_ge(st_ready, G)
            nc.tensor.matmul(st_p[0:1, 0, 0:1], inexact[:], ones[:], start=True, stop=True).then_inc(inexact_made, 1)
            pe.wait_ge(wo_loaded, 16)
            pe.wait_ge(q_ready, G)
            pe.wait_ge(k_ready, G)
            for g in range(G):
                pe.wait_ge(cx_ready, g + 1)
                for a in range(LT):
                    last = nc.tensor.matmul(qk_p[a][:], cT[:, g, a * P:(a + 1) * P], wo_sb[:, g, :],
                                            start=g == 0, stop=g == G - 1)
                    if g == G - 1:
                        last.then_inc(out_made, 1)
            transposed(LT)


U1 = 2 * HID // (2 * 2 * P)
UH = KH
U3 = KH // 4
RING = 4
AHEAD = 2
UNITS = U1 + 2 * UH + U3
PIECE = 512
PIECES = UNITS * UNIT // PIECE
FIRST = {1: 0, 2: U1, 3: U1 + UH, 4: U1 + 2 * UH}
TILE0 = {1: 0, 2: KH, 3: 2 * KH}
assert not any(n % RING for n in FIRST.values()) and U3 == RING


def units(engine, one):
    for i in range(U1 // RING):
        for q in range(RING):
            one(1, i, q)
    for layer in (2, 3):
        with engine.Fori(0, UH // RING) as i:
            for q in range(RING):
                one(layer, i, q)
    for q in range(RING):
        one(4, 0, q)


def mlp(nc, w_all, scales, s3, out, keep):
    x2, xT_psum, raw, raw_loaded = keep["x2"], keep["xT_psum"], keep["raw"], keep["raw_loaded"]
    w_hi, w_lo, w_rounded, w_split = keep["w_hi"], keep["w_lo"], keep["w_rounded"], keep["w_split"]
    with ExitStack() as stack:
        def sb(name, shape, dt=F32):
            return stack.enter_context(nc.sbuf_tensor(name, shape, dt))

        def sem(name):
            return stack.enter_context(nc.semaphore(name))

        h_hi = [sb(f"h_hi{i}", [P, KH, L], F32R) for i in range(2)]
        h_lo = [sb(f"h_lo{i}", [P, KH, L], F32R) for i in range(2)]
        hf, gate = sb("hf", [P, 2, L]), sb("gate", [P, 2, L])
        scale = sb("scales", [P, 4, KH])
        s3_sb, y = sb("s3_sb", [P, E]), sb("y", [P, LT, E])
        ps = [stack.enter_context(nc.psum_tensor(f"ps{i}", [P, 2, L], F32)) for i in range(4)]
        py = [stack.enter_context(nc.psum_tensor(f"py{i}", [P, E], F32)) for i in range(LT)]

        scales_loaded, stored = sem("scales_ld"), sem("stored")
        sums_ready, act_ready, hf_ready = sem("sums_ready"), sem("act_ready"), sem("hf_ready")
        h_rounded, h_ready = sem("h_rounded"), sem("h_ready")
        x_rounded, x_split, y_step, y_ready = sem("x_rounded"), sem("x_split"), sem("y_step"), sem("y_ready")
        y_made = sem("y_made")
        block = stack.enter_context(nc.Block())

        @block.sync
        def _(sp):
            for i, s in enumerate(scales):
                sp.dma_start(scale[:, i, :], s).then_inc(scales_loaded, 16)
            sp.dma_start(s3_sb[:], s3.partition_broadcast(P)).then_inc(scales_loaded, 16)

            def one(layer, i, q):
                if layer == 1 and i == 0:
                    return
                sp.wait_ge(w_split, i * RING + (FIRST[layer] + q - RING + 1))
                sp.dma_start(raw[:, q, :], w_all[i * RING + (FIRST[layer] + q)]).then_inc(raw_loaded[q], 16)

            units(sp, one)
            for a in range(LT):
                sp.wait_ge(y_ready, a + 1)
                sp.dma_start(out[0, a * P:(a + 1) * P, :], y[:, a, :]).then_inc(stored, 16)
            sp.wait_ge(stored, 16 * LT)

        @block.scalar
        def _(act):
            act.wait_ge(scales_loaded, 16 * 5)

            def w_round(layer, i, q):
                at = (q + AHEAD) % RING
                act.wait_ge(raw_loaded[at], i * 16 + 16 * (FIRST[layer] // RING + (q + AHEAD) // RING + 1))
                u = i * RING + (FIRST[layer] + q + AHEAD)
                if layer == 1 and u >= RING:
                    act.wait_ge(sums_ready, 2 * (u - RING + 1))
                elif layer > 1:
                    act.wait_ge(sums_ready, u + (U1 - RING + 1))
                nc.scalar.activation(w_hi[:, at, :], raw[:, at, :], ACT.Copy).then_inc(w_rounded, 1)

            def one(layer, i, q):
                if not (layer == 4 and q + AHEAD >= U3):
                    w_round(layer, i, q)
                if layer == 1:
                    for n in (2 * (i * RING + q), 2 * (i * RING + q) + 1):
                        act.wait_ge(sums_ready, n + 1)
                        if n >= 2:
                            act.wait_ge(hf_ready, n - 1)
                        nc.scalar.activation(gate[:, n % 2, :], ps[n % 4][:, 0, :], ACT.Silu,
                                             scale=scale[:, 0, n:n + 1]).then_inc(act_ready, 1)
                elif layer < 4:
                    n = i * RING + (TILE0[layer] + q)
                    act.wait_ge(sums_ready, n + 1)
                    act.wait_ge(h_ready, n - 1)
                    nc.scalar.activation(hf[:, q % 2, :], ps[q][:, 0, :], ACT.Gelu,
                                         scale=scale[:, layer, bass.ds(i * RING + q, 1)]).then_inc(act_ready, 1)

            units(act, one)

        @block.vector
        def _(dve):
            for a in range(LT):
                cols, made = slice(a * P, (a + 1) * P), xT_psum[:, a, :].rearrange("p (k l) -> p k l", k=KE)
                nc.vector.tensor_copy(h_hi[1][:, 0:KE, cols], made).then_inc(x_rounded, 1)
                dve.wait_ge(x_rounded, a + 1)
                nc.vector.tensor_tensor(h_lo[1][:, 0:KE, cols], made, f32(h_hi[1][:, 0:KE, cols]),
                                        ALU.subtract).then_inc(x_split, 1)
            dve.wait_ge(scales_loaded, 16 * 5)

            def hidden(exact):
                def w_rest(layer, i, q):
                    at = (q + AHEAD) % RING
                    dve.wait_ge(w_rounded, i * RING + (FIRST[layer] + q + AHEAD + 1))
                    n = 1 if exact else UNIT
                    nc.vector.tensor_tensor(w_lo[:, at, 0:n], raw[:, at, 0:n], f32(w_hi[:, at, 0:n]),
                                            ALU.subtract).then_inc(w_split, 1)

                def h_split(n, o, slot, to):
                    nc.vector.tensor_copy(h_hi[to][:, bass.ds(o, 1), :], hf[:, slot:slot + 1, :]).then_inc(h_rounded, 1)
                    dve.wait_ge(h_rounded, n + 1)
                    nc.vector.tensor_tensor(h_lo[to][:, bass.ds(o, 1), :], hf[:, slot:slot + 1, :],
                                            f32(h_hi[to][:, bass.ds(o, 1), :]), ALU.subtract).then_inc(h_ready, 1)

                def one(layer, i, q):
                    if not (layer == 4 and q + AHEAD >= U3):
                        w_rest(layer, i, q)
                    if layer == 1:
                        for n in (2 * (i * RING + q), 2 * (i * RING + q) + 1):
                            dve.wait_ge(act_ready, n + 1)
                            if n >= 2:
                                dve.wait_ge(h_ready, n - 1)
                            nc.vector.scalar_tensor_tensor(out=hf[:, n % 2, :], in0=ps[n % 4][:, 1, :],
                                                           scalar=scale[:, 1, n:n + 1], in1=gate[:, n % 2, :],
                                                           op0=ALU.mult, op1=ALU.mult).then_inc(hf_ready, 1)
                            dve.wait_ge(hf_ready, n + 1)
                            h_split(n, n, n % 2, 0)
                    elif layer < 4:
                        n = i * RING + (TILE0[layer] + q)
                        dve.wait_ge(act_ready, n + 1)
                        h_split(n, i * RING + q, q % 2, layer % 2 ^ 1)

                units(dve, one)

            dve.wait_ge(keep["inexact_ready"], 1)
            count = nc.vector.value_load(keep["any_inexact"][:], min_val=0, max_val=P)
            with dve.If(count > 0):
                hidden(exact=False)
            with dve.Else():
                hidden(exact=True)
            for a in range(LT):
                dve.wait_ge(y_made, a + 1)
                nc.vector.tensor_tensor(y[:, a, :], py[a][:], s3_sb[:], ALU.mult).then_inc(y_step, 1)
                dve.wait_ge(y_step, a + 1)
                nc.vector.tensor_tensor(y[:, a, :], y[:, a, :], x2[:, a, :], ALU.add).then_inc(y_ready, 1)

        @block.tensor
        def _(pe):
            pe.wait_ge(x_split, LT)

            def multiply(exact):
                def terms(w_hi, w_lo, x_hi, x_lo):
                    return ((w_hi, x_hi), (w_hi, x_lo)) if exact else ((w_hi, x_hi), (w_lo, x_hi), (w_hi, x_lo))

                passes = 2 if exact else 3

                def one(layer, i, q):
                    pe.wait_ge(w_split, i * RING + (FIRST[layer] + q + 1))
                    if layer == 1:
                        hi = w_hi[:, q, :].rearrange("p (w o k n) -> p w o k n", w=2, o=2, k=KE)
                        lo = w_lo[:, q, :].rearrange("p (w o k n) -> p w o k n", w=2, o=2, k=KE)
                        for o in range(2):
                            n = 2 * (i * RING + q) + o
                            if n >= 4:
                                pe.wait_ge(hf_ready, n - 3)
                            for w in range(2):
                                m = 0
                                for wt, x in terms(hi, lo, h_hi[1], h_lo[1]):
                                    for k in range(KE):
                                        last = nc.tensor.matmul(ps[n % 4][:, w, :], wt[:, w, o, k, :], x[:, k, :],
                                                                start=m == 0, stop=m == passes * KE - 1)
                                        m += 1
                            last.then_inc(sums_ready, 1)
                    elif layer < 4:
                        hi = w_hi[:, q, :].rearrange("p (k n) -> p k n", k=KH)
                        lo = w_lo[:, q, :].rearrange("p (k n) -> p k n", k=KH)
                        src = layer % 2
                        pe.wait_ge(act_ready, i * RING + (TILE0[layer] + q - 3))
                        m = 0
                        for tiles in (range(KH - 2), range(KH - 2, KH)):
                            pe.wait_ge(h_ready, TILE0[layer] - KH + tiles.stop)
                            for wt, x in terms(hi, lo, h_hi[src], h_lo[src]):
                                for k in tiles:
                                    last = nc.tensor.matmul(ps[q][:, 0, :], wt[:, k, :], x[:, k, :],
                                                            start=m == 0, stop=m == passes * KH - 1)
                                    m += 1
                        last.then_inc(sums_ready, 1)
                    else:
                        hi = w_hi[:, q, :].rearrange("p (k n) -> p k n", k=4)
                        lo = w_lo[:, q, :].rearrange("p (k n) -> p k n", k=4)
                        pe.wait_ge(h_ready, 2 * KH + 4 * q + 4)
                        for a in range(LT):
                            rows = slice(a * P, (a + 1) * P)
                            m = 0
                            for wt, x in terms(hi, lo, h_hi[0], h_lo[0]):
                                for k in range(4):
                                    last = nc.tensor.matmul(py[a][:], x[:, 4 * q + k, rows], wt[:, k, :],
                                                            start=q == 0 and m == 0,
                                                            stop=q == U3 - 1 and m == passes * 4 - 1)
                                    m += 1
                            if q == U3 - 1:
                                last.then_inc(y_made, 1)

                units(pe, one)

            pe.wait_ge(keep["inexact_ready"], 1)
            count = nc.tensor.value_load(keep["any_inexact"][:], min_val=0, max_val=P)
            with pe.If(count > 0):
                multiply(exact=False)
            with pe.Else():
                multiply(exact=True)


def build(nc, x, ctxT, wqT, wkT, wvT, woT, wqk, bqk, wv, bv, wn, bn, wo, bo,
          w_all, s1, s2, sh1, sh2, s3, out):
    with ExitStack() as stack:
        def sb(name, shape, dt=F32):
            return stack.enter_context(nc.sbuf_tensor(name, shape, dt))

        keep = {"ident": sb("ident", [P, P]), "x1": sb("x1", [P, LT, E])}
        keep["exact"] = sb("exact", [P, PIECE])
        cross_attention(nc, x, ctxT, wqT, wkT, wvT, woT, w_all, keep)
        keep |= {"any_inexact": sb("any_inexact", [1, 1], mybir.dt.int32),
                 "inexact_ready": stack.enter_context(nc.semaphore("any_inexact_ready")),
                 "x2": sb("x2", [P, LT, E]), "raw": sb("w_raw", [P, RING, UNIT]),
                 "w_hi": sb("w_hi", [P, RING, UNIT], F32R), "w_lo": sb("w_lo", [P, RING, UNIT], F32R),
                 "xT_psum": stack.enter_context(nc.psum_tensor("xT_psum", [P, LT, E], F32)),
                 "raw_loaded": [stack.enter_context(nc.semaphore(f"raw_loaded{q}")) for q in range(RING)],
                 "w_rounded": stack.enter_context(nc.semaphore("w_rounded")),
                 "w_split": stack.enter_context(nc.semaphore("w_split"))}
        self_attention(nc, wqk, bqk, wv, bv, wn, bn, wo, bo, w_all, keep)
        mlp(nc, w_all, (s1, s2, sh1, sh2), s3, out, keep)


def kernel(**inputs):
    from concourse import bacc
    from concourse.bass_utils import run_bass_kernel_spmd

    a = {k: np.asarray(v) for k, v in inputs.items()}

    def rows_split(w):
        return w.reshape(-1, P, w.shape[1]).transpose(1, 0, 2)

    def out_tiles(w):
        return w.reshape(w.shape[0] // P, P, w.shape[1] // P, P).transpose(0, 3, 2, 1)

    w1, w2 = (out_tiles(a[f"L0_ffn_{n}_w"]).reshape(U1, 2, P, KE * P).transpose(0, 2, 1, 3) for n in ("w1", "w2"))
    arrays = {
        "x": a["x"],
        "ctxT": a["ctx_1024"][0].reshape(NC, CH, KE, P).transpose(0, 3, 2, 1),
        "wqT": rows_split(a["L0_xattn_Wq"].T),
        "wkT": rows_split(a["L0_xattn_Wk"].T),
        "wvT": rows_split(a["L0_xattn_Wv"].T),
        "woT": rows_split(a["L0_xattn_Wo"].T),
        "wqk": rows_split(a["L0_attn_Wqk"]),
        "bqk": a["L0_attn_bqk"].reshape(2 * KE, P).T,
        "wv": rows_split(a["L0_attn_Wv"]), "bv": a["L0_attn_bv"],
        "wn": rows_split(a["L0_attn_Wn"]), "bn": a["L0_attn_bn"].reshape(H, 1),
        "wo": rows_split(a["L0_attn_Wo"]), "bo": a["L0_attn_bo"],
        "w_all": np.concatenate([
            np.stack([w1, w2], axis=2).reshape(U1, P, UNIT),
            out_tiles(a["L0_ffn_h1_w"]).reshape(UH, P, UNIT),
            out_tiles(a["L0_ffn_h2_w"]).reshape(UH, P, UNIT),
            a["L0_ffn_w3_w"].T.reshape(U3, 4, P, E).transpose(0, 2, 1, 3).reshape(U3, P, UNIT)]),
        "s1": a["L0_ffn_w1_s"].reshape(KH, P).T, "s2": a["L0_ffn_w2_s"].reshape(KH, P).T,
        "sh1": a["L0_ffn_h1_s"].reshape(KH, P).T, "sh2": a["L0_ffn_h2_s"].reshape(KH, P).T,
        "s3": a["L0_ffn_w3_s"],
    }
    arrays = {f"{k}_dram": np.ascontiguousarray(v) for k, v in arrays.items()}
    nc = bacc.Bacc("TRN2", target_bir_lowering=False, num_devices=1)
    aps = [nc.dram_tensor(k, v.shape, mybir.dt.from_np(v.dtype), kind="ExternalInput").ap()
           for k, v in arrays.items()]
    out = nc.dram_tensor("out_dram", (1, L, E), F32, kind="ExternalOutput").ap()
    build(nc, *aps, out)
    result = run_bass_kernel_spmd(nc, [arrays], core_ids=[0])
    return result.results[0]["out_dram"]
```

```python
from contextlib import ExitStack

import numpy as np

import concourse.bass as bass
from concourse import mybir

F32 = mybir.dt.float32
F32R = mybir.dt.float32r
BF16 = mybir.dt.bfloat16
ALU = mybir.AluOpType
ACT = mybir.ActivationFunctionType

P = 128
L = 256
E = 512
S = 25088
H = 16
D = E // H
HID = 2048
KE = E // P
KH = HID // P
LT = L // P
HG = P // D
G = H // HG
CH = 512
NC = S // CH
TC = CH // P
EPS = 1e-5
UNIT = KH * P
assert NC * CH == S and G == TC == KE


def f32(ap):
    return ap.bitcast(F32)


class Chain:

    def __init__(self, engine, sem):
        self.engine, self.sem, self.n = engine, sem, 0

    def add(self, instruction):
        self.n += 1
        instruction.then_inc(self.sem, 1)
        return self.n

    def wait(self, n):
        self.engine.wait_ge(self.sem, n)


class Layernorm:

    def __init__(self, nc, dve, x, xn, stats, mv, chain, var_ready, sd_ready, done, xn_ready):
        self.nc, self.dve, self.x, self.xn, self.stats, self.mv = nc, dve, x, xn, stats, mv
        self.chain, self.var_ready, self.sd_ready, self.done, self.xn_ready = chain, var_ready, sd_ready, done, xn_ready

    def moments(self, a):
        nc, mv = self.nc, self.mv
        self.chain.wait(self.chain.add(nc.vector.bn_stats(self.stats[:, a, :], self.x[:, a, :])))
        self.chain.wait(self.chain.add(nc.vector.bn_aggr(mv[:, a, 0:2], self.stats[:, a, :])))
        nc.vector.tensor_scalar_add(mv[:, a, 2:3], mv[:, a, 1:2], EPS).then_inc(self.var_ready, 1)

    def normalised(self, a):
        nc, mv = self.nc, self.mv
        self.dve.wait_ge(self.sd_ready, self.done + a + 1)
        self.chain.wait(self.chain.add(nc.vector.reciprocal(mv[:, a, 3:4], mv[:, a, 2:3])))
        nc.vector.tensor_scalar(self.xn[:, a, :], self.x[:, a, :], mv[:, a, 0:1], mv[:, a, 3:4],
                                ALU.subtract, ALU.mult).then_inc(self.xn_ready, 1)


def roots(nc, act, mv, var_ready, sd_ready, done):
    for a in range(LT):
        act.wait_ge(var_ready, done + a + 1)
        nc.scalar.activation(mv[:, a, 2:3], mv[:, a, 2:3], ACT.Sqrt).then_inc(sd_ready, 1)


def table(nc, keep, function):
    one = keep["one"]
    keep["tables"] += 1
    nc.scalar.activation(one[:, keep["tables"]:keep["tables"] + 1], one[:, 0:1], function)


def keep_clock(nc, keep, to, n):
    zeros = keep["zeros"]
    for _ in range(n):
        nc.tensor.matmul(to, zeros[:, 0:P], zeros[:], start=True, stop=True, skip_group_check=True)


def cross_attention(nc, x, ctxT, wqT, wkT, wvT, woT, wqk, wv, bv, wo, w_all, keep):
    ident, x1, qst, next_weights = keep["ident"], keep["x1"], keep["rows"][0], keep["weights"][1]
    with ExitStack() as stack:
        def sb(name, shape, dt=F32):
            return stack.enter_context(nc.sbuf_tensor(name, shape, dt))

        def sem(name):
            return stack.enter_context(nc.semaphore(name))

        wk_hi, wk_lo, wv_hi, wv_lo = (keep["weights"][0][:, i, :, :] for i in range(4))
        raw = sb("ctx_raw", [P, KE, CH])
        c_hi, c_lo = sb("c_hi", [P, 2, KE, CH], F32R), sb("c_lo", [P, 2, KE, CH], F32R)
        kst = sb("k_stack", [P, 2, HG, G, CH], F32R)
        v = sb("v", [P, 2, E])
        probs = sb("probs", [P, 2, G, HG * L])
        stats, mv = sb("ln_stats", [P, LT, 6]), sb("ln_mv", [P, LT, 4])
        zeros = keep["zeros"]
        piece, piece_hi = sb("piece", [P, 2, PIECE]), sb("piece_hi", [P, PIECE], F32R)
        rest = sb("rest", [P, PIECE])
        exact, zero, unused = keep["exact"], sb("zero", [P, 1]), sb("unused", [P, 1])
        oT, wo_sb = v[:, :, :].rearrange("p a n -> p (a n)").rearrange("p (g l) -> p g l", g=G), raw
        wk_raw = probs[:, 0, 0:2, :].rearrange("p a b -> p (a b)").rearrange("p (k n) -> p k n", k=KE)
        wv_raw = probs[:, 0, 2:4, :].rearrange("p a b -> p (a b)").rearrange("p (k n) -> p k n", k=KE)
        wq_raw = probs[:, 1, 2:4, :].rearrange("p a b -> p (a b)").rearrange("p (k n) -> p k n", k=KE)
        x_sb = probs[:, 1, 0, :].rearrange("p (a n) -> p a n", a=LT)
        xn = probs[:, 1, 1, :].rearrange("p (a n) -> p a n", a=LT)
        xnT = v[:, :, :].rearrange("p a n -> p (a n)").rearrange("p (k l) -> p k l", k=KE)

        sc = [stack.enter_context(nc.psum_tensor(f"sc{i}", [P, HG * L], F32)) for i in range(2)]
        kp = stack.enter_context(nc.psum_tensor("kp", [P, CH], F32))
        vp = stack.enter_context(nc.psum_tensor("vp", [P, E], F32))
        acc = stack.enter_context(nc.psum_tensor("acc", [P, G, L], F32))

        x_loaded, wq_loaded, wo_loaded = sem("x_loaded"), sem("wq_loaded"), sem("wox_loaded")
        wk_loaded, wv_loaded, ctx_loaded = sem("wk_loaded"), sem("wv_loaded"), sem("ctx_loaded")
        ident_zero, const_ready, chain = sem("ident_zero"), sem("const_ready"), sem("dve_chain")
        var_ready, sd_ready, xn_ready = sem("var_ready"), sem("sd_ready"), sem("xn_ready")
        xnT_made, xnT_ready, q_made = sem("xnT_made"), sem("xnT_ready"), sem("q_made")
        one_ready, zeros_ready = sem("one_ready"), sem("zeros_ready")
        xn1_ready, xn1T_made, xn1T_ready = sem("xn1_ready"), sem("xn1T_made"), sem("xn1T_ready")
        bv_loaded, v1_made, v1_ready = sem("bv_loaded"), sem("v1_made"), sem("v1_ready")
        q_hi, q_lo, q_dup = sem("q_hi"), sem("q_lo"), sem("q_dup")
        wk_hi_done, wv_hi_done = sem("wk_hi_done"), sem("wv_hi_done")
        wk_split, wv_split = sem("wk_split"), sem("wv_split")
        ctx_hi, ctx_split = sem("ctx_hi"), sem("ctx_split")
        k_made, k_hi, k_lo, k_dup = sem("k_made"), sem("k_hi"), sem("k_lo"), sem("k_dup")
        k_dup0 = [sem(f"k_dup_of_first{g}") for g in range(G)]
        v_made, v_ready = sem("v_made"), sem("v_ready")
        scores_ready, probs_ready, probs_used = sem("scores_ready"), sem("probs_ready"), sem("probs_used")
        piece_loaded = [sem(f"piece_loaded{i}") for i in range(2)]
        scan_ready, piece_rounded, piece_used = sem("scan_ready"), sem("piece_rounded"), sem("piece_used")
        rest_compared, exact_counted = sem("rest_compared"), sem("exact_counted")
        o_saved, o_projected, x1_ready = sem("o_saved"), sem("o_projected"), sem("x1_ready")
        block = stack.enter_context(nc.Block())
        x_rows = x[0].rearrange("(a p) n -> p a n", p=P)
        SCALE = float(D) ** -0.5

        def q_of(j):
            return sc[0][D * j:D * (j + 1), :].rearrange("p (g l) -> p g l", g=G)

        k_first = (kp[:], vp[:], acc[:, 0:2, :].rearrange("p g l -> p (g l)"),
                   acc[:, 2:4, :].rearrange("p g l -> p (g l)"))

        LOOPED = (NC - 5) // 2 * 2
        assert LOOPED == UNITS and UNIT == TC * PIECE

        def chunks(engine, one):
            def flags(c):
                return c == 0, c + 1 < NC, c + 2 < NC, c + 3 < NC, False
            one(0, 0, *flags(0))
            with engine.Fori(0, LOOPED // 2) as i:
                one(i * 2 + 1, 1, False, True, True, True, True)
                one(i * 2 + 2, 0, False, True, True, True, True)
            for c in range(LOOPED + 1, NC):
                one(c, c % 2, *flags(c))

        @block.sync
        def _(sp):
            sp.dma_start(x_sb, x_rows).then_inc(x_loaded, 16)
            sp.dma_start(wq_raw, wqT).then_inc(wq_loaded, 16)
            sp.dma_start(wk_raw, wkT).then_inc(wk_loaded, 16)
            sp.dma_start(raw[:], ctxT[0]).then_inc(ctx_loaded, 16)
            sp.dma_start(wv_raw, wvT).then_inc(wv_loaded, 16)
            sp.wait_ge(ctx_split, 1)
            sp.dma_start(raw[:], ctxT[1]).then_inc(ctx_loaded, 16)
            for j in range(HG):
                sp.wait_ge(q_hi, j + 1)
                sp.dma_start(f32(qst[D:2 * D, j, :, :]), f32(qst[0:D, j, :, :])).then_inc(q_dup, 16)
            for g in range(G):
                sp.wait_ge(k_hi, (g + 1) * HG)
                sp.dma_start(f32(kst[2 * D:3 * D, 0, :, g, :]), f32(kst[0:D, 0, :, g, :])).then_inc(k_dup0[g], 16)
            sp.wait_ge(ctx_split, 2)
            sp.dma_start(raw[:], ctxT[2]).then_inc(ctx_loaded, 16)
            sp.dma_start(x1[:], x_rows).then_inc(x_loaded, 16)
            for n in range(2):
                sp.dma_start(piece[:, n, :], w_all[0][:, n * PIECE:(n + 1) * PIECE]).then_inc(piece_loaded[n], 16)

            def one(c, par, first, k_next, split_next, load_next, looped):
                if load_next:
                    sp.wait_ge(ctx_split, c + 3)
                    sp.dma_start(raw[:], ctxT[c + 3]).then_inc(ctx_loaded, 16)
                if looped:
                    for n in range(2, TC + 2):
                        u = c - 1 if n < TC else c % UNITS
                        sp.wait_ge(piece_used, c * TC + (n - 2 - TC + 1))
                        sp.dma_start(piece[:, n % 2, :], w_all[u][:, n % TC * PIECE:(n % TC + 1) * PIECE]
                                     ).then_inc(piece_loaded[n % 2], 16)

            chunks(sp, one)
            sp.wait_ge(ctx_split, NC)
            sp.dma_start(wo_sb[:], woT).then_inc(wo_loaded, 16)
            sp.wait_ge(k_made, NC * G)
            sp.dma_start(next_weights[:, 0, :, :], wv).then_inc(keep["wv_loaded"], 16)
            sp.dma_start(next_weights[:, 1, :, :], wqk[:, :, 0:E]).then_inc(keep["wqk_loaded"], 16)
            sp.wait_ge(exact_counted, UNITS * TC)
            sp.dma_start(rest[:], bv.partition_broadcast(P)).then_inc(bv_loaded, 16)
            sp.wait_ge(v_made, NC * TC)
            sp.dma_start(next_weights[:, 2, :, :], wqk[:, :, E:2 * E]).then_inc(keep["wqk_loaded"], 16)
            sp.dma_start(next_weights[:, 3, :, :], wo).then_inc(keep["wo_loaded"], 16)

        @block.gpsimd
        def _(pool):
            nc.gpsimd.memset(keep["one"][:, 0:1], 1.0).then_inc(one_ready, 1)
            nc.gpsimd.memset(zeros[:], 0.0).then_inc(zeros_ready, 1)
            nc.gpsimd.memset(zero[:], 0.0).then_inc(one_ready, 1)
            nc.gpsimd.memset(ident[:], 0.0).then_inc(ident_zero, 1)
            pool.wait_ge(ident_zero, 1)
            nc.gpsimd.affine_select(out=ident[:], in_=ident[:], compare_op=ALU.not_equal, fill=1.0,
                                    base=0, pattern=[[-1, P]], channel_multiplier=1).then_inc(const_ready, 1)
            pool.wait_ge(one_ready, 2)
            pool.wait_ge(wv_hi_done, 1)
            nc.gpsimd.tensor_tensor(wv_lo, wv_raw, f32(wv_hi), ALU.subtract).then_inc(wv_split, 1)
            pool.wait_ge(wv_split, 1)
            pool.wait_ge(ctx_loaded, 32)
            nc.gpsimd.tensor_tensor(c_hi[:, 1, :, :], raw[:], zero[:].unsqueeze(2).to_broadcast([P, KE, CH]),
                                    ALU.add).then_inc(ctx_hi, 1)
            pool.wait_ge(ctx_hi, 2)
            nc.gpsimd.tensor_tensor(c_lo[:, 1, :, :], raw[:], f32(c_hi[:, 1, :, :]), ALU.subtract).then_inc(ctx_split, 1)
            pool.wait_ge(ctx_split, 2)
            nc.gpsimd.memset(exact[:], 0.0).then_inc(scan_ready, 1)
            pool.wait_ge(scan_ready, 1)

            with pool.Fori(0, UNITS) as u:
                for t in range(TC):
                    n = u * TC + t
                    pool.wait_ge(piece_loaded[t % 2], u * (TC // 2 * 16) + (t // 2 + 1) * 16)
                    nc.gpsimd.tensor_tensor(piece_hi[:], piece[:, t % 2, :], zero[:].to_broadcast([P, PIECE]), ALU.add
                                            ).then_inc(piece_rounded, 1)
                    pool.wait_ge(piece_rounded, n + 1)
                    nc.gpsimd.tensor_tensor(rest[:], piece[:, t % 2, :], f32(piece_hi[:]),
                                            ALU.subtract).then_inc(piece_used, 1)
                    pool.wait_ge(piece_used, n + 1)
                    nc.gpsimd.tensor_tensor(unused[:], zero[:], zero[:], ALU.add)
                    nc.gpsimd.tensor_scalar(rest[:], rest[:], 0.0, None, ALU.is_equal).then_inc(rest_compared, 1)
                    pool.wait_ge(rest_compared, n + 1)
                    nc.gpsimd.tensor_tensor(exact[:], exact[:], rest[:], ALU.add).then_inc(exact_counted, 1)
                    pool.wait_ge(exact_counted, n + 1)

        @block.scalar
        def _(act):
            act.wait_ge(one_ready, 1)
            table(nc, keep, ACT.Sqrt)
            roots(nc, act, mv, var_ready, sd_ready, 0)
            for a in range(LT):
                act.wait_ge(xnT_made, a + 1)
                nc.scalar.activation(xnT[:, :, a * P:(a + 1) * P], sc[1][:, a * E:(a + 1) * E].rearrange(
                    "p (k l) -> p k l", k=KE), ACT.Copy).then_inc(xnT_ready, 1)
            table(nc, keep, ACT.Sigmoid)

            def k_rows(u, par, g, source):
                act.wait_ge(k_made, u + 1)
                for j in range(HG):
                    nc.scalar.activation(kst[0:D, par, j, g, :], source[D * j:D * (j + 1), :],
                                         ACT.Copy).then_inc(k_hi, 1)

            def sigmoid(n, tile, t, g, first):
                act.wait_ge(scores_ready, n + 1)
                if not (first and t < 2):
                    act.wait_ge(probs_used, tile - 1)
                nc.scalar.activation(probs[:, t % 2, g, :], sc[g % 2][:], ACT.Sigmoid).then_inc(probs_ready, 1)

            def rounded(hi, source, loaded, count, done):
                act.wait_ge(loaded, count)
                nc.scalar.activation(hi, source, ACT.Copy).then_inc(done, 1)

            rounded(wk_hi, wk_raw, wk_loaded, 16, wk_hi_done)
            rounded(c_hi[:, 0, :, :], raw[:], ctx_loaded, 16, ctx_hi)
            rounded(wv_hi, wv_raw, wv_loaded, 16, wv_hi_done)
            act.wait_ge(q_made, 1)
            for j in range(HG):
                nc.scalar.activation(qst[0:D, j, :, :], q_of(j), ACT.Copy, scale=SCALE).then_inc(q_hi, 1)
            for g in range(G):
                k_rows(g, 0, g, k_first[g])

            def one(c, par, first, k_next, split_next, load_next, looped):
                for t in range(TC):
                    tile = c * TC + t
                    for g in (0, 1):
                        sigmoid(tile * G + g, tile, t, g, first)
                    if k_next:
                        k_rows(tile + TC, 1 - par, t, kp[:])
                    for g in (2, 3):
                        sigmoid(tile * G + g, tile, t, g, first)

            chunks(act, one)
            table(nc, keep, ACT.Sqrt)
            roots(nc, act, mv, var_ready, sd_ready, LT)
            table(nc, keep, ACT.Exp)

        @block.vector
        def _(dve):
            own = Chain(dve, chain)
            norm = Layernorm(nc, dve, x_sb, xn, stats, mv, own, var_ready, sd_ready, 0, xn_ready)
            dve.wait_ge(x_loaded, 16)
            for a in range(LT):
                norm.moments(a)
            for a in range(LT):
                norm.normalised(a)

            def split_chunk(c, par):
                dve.wait_ge(ctx_loaded, 16 * c + 16)
                nc.vector.tensor_copy(c_hi[:, par, :, :], raw[:]).then_inc(ctx_hi, 1)
                dve.wait_ge(ctx_hi, c + 1)
                nc.vector.tensor_tensor(c_lo[:, par, :, :], raw[:], f32(c_hi[:, par, :, :]),
                                        ALU.subtract).then_inc(ctx_split, 1)

            def k_rest(u, par, g, source, copied=False):
                for j in range(HG):
                    dve.wait_ge(k_hi, u * HG + j + 1)
                    nc.vector.tensor_tensor(kst[D:2 * D, par, j, g, :], source[D * j:D * (j + 1), :],
                                            f32(kst[0:D, par, j, g, :]), ALU.subtract).then_inc(k_lo, 1)
                if not copied:
                    nc.vector.tensor_copy(kst[2 * D:3 * D, par, :, g, :],
                                          kst[0:D, par, :, g, :]).then_inc(k_dup, 1)

            def v_out(m, buf, free):
                dve.wait_ge(v_made, m + 1)
                if free:
                    dve.wait_ge(probs_used, m - 1)
                nc.vector.tensor_copy(v[:, buf, :], vp[:]).then_inc(v_ready, 1)

            dve.wait_ge(wk_hi_done, 1)
            nc.vector.tensor_tensor(wk_lo, wk_raw, f32(wk_hi), ALU.subtract).then_inc(wk_split, 1)
            dve.wait_ge(ctx_hi, 1)
            nc.vector.tensor_tensor(c_lo[:, 0, :, :], raw[:], f32(c_hi[:, 0, :, :]), ALU.subtract).then_inc(ctx_split, 1)
            for j in range(HG):
                dve.wait_ge(q_hi, j + 1)
                nc.vector.scalar_tensor_tensor(out=qst[2 * D:3 * D, j, :, :], in0=q_of(j), scalar=SCALE,
                                               in1=f32(qst[0:D, j, :, :]), op0=ALU.mult,
                                               op1=ALU.subtract).then_inc(q_lo, 1)
            for g in range(G):
                k_rest(g, 0, g, k_first[g], copied=True)
            v_out(0, 0, False)

            def one(c, par, first, k_next, split_next, load_next, looped):
                for t in range(TC):
                    tile = c * TC + t
                    if t == TC - 1 and split_next:
                        dve.wait_ge(v_made, tile + 1)
                        split_chunk(c + 2, par)
                    if k_next:
                        k_rest(tile + TC, 1 - par, t, kp[:])
                    if k_next or t < TC - 1:
                        v_out(tile + 1, (t + 1) % 2, not (first and t == 0))

            chunks(dve, one)
            dve.wait_ge(probs_used, NC * TC)
            for g in range(G):
                nc.vector.tensor_copy(oT[:, g, :], acc[:, g, :]).then_inc(o_saved, 1)
            dve.wait_ge(x_loaded, 32)
            norm = Layernorm(nc, dve, x1, keep["xn"], stats, mv, own, var_ready, sd_ready, LT, xn1_ready)

            def transposed(a):
                dve.wait_ge(xn1T_made, a + 1)
                nc.vector.tensor_copy(keep["xnT"][:, :, a * P:(a + 1) * P],
                                      sc[0][:, a * E:(a + 1) * E].rearrange("p (k l) -> p k l", k=KE)
                                      ).then_inc(xn1T_ready, 1)

            for a, projected in enumerate((kp, vp)):
                dve.wait_ge(o_projected, a + 1)
                nc.vector.tensor_tensor(x1[:, a, :], x1[:, a, :], projected[:], ALU.add).then_inc(x1_ready, 1)
                dve.wait_ge(x1_ready, a + 1)
                norm.moments(a)
                norm.normalised(a)
                transposed(a)
            dve.wait_ge(bv_loaded, 16)
            for a, made in enumerate((kp, vp)):
                dve.wait_ge(v1_made, a + 1)
                nc.vector.tensor_tensor(keep["v"][:, a, :], made[:], rest[:], ALU.add).then_inc(v1_ready, 1)
            dve.wait_ge(v1_ready, LT)

        @block.tensor
        def _(pe):
            pe.wait_ge(zeros_ready, 1)
            keep_clock(nc, keep, kp[:], 14)
            pe.wait_ge(const_ready, 1)
            for a in range(LT):
                pe.wait_ge(xn_ready, a + 1)
                for k in range(KE):
                    last = nc.tensor.transpose(sc[1][:, a * E + k * P:a * E + (k + 1) * P],
                                               xn[:, a, k * P:(k + 1) * P], ident[:])
                last.then_inc(xnT_made, 1)
            keep_clock(nc, keep, kp[:], 3)
            pe.wait_ge(wq_loaded, 16)
            pe.wait_ge(xnT_ready, LT)
            for g in range(G):
                for k in range(KE):
                    last = nc.tensor.matmul(sc[0][:, g * L:(g + 1) * L], wq_raw[:, k, g * P:(g + 1) * P],
                                            xnT[:, k, :], start=k == 0, stop=k == KE - 1)
            last.then_inc(q_made, 1)

            def k_project(u, par, g, to, free, before=((), (), ())):
                if free:
                    pe.wait_ge(k_lo, u * HG)
                n = 0
                for i, (w, c) in enumerate(((wk_hi, c_hi), (wk_lo, c_hi), (wk_hi, c_lo))):
                    for ready, count in before[i]:
                        pe.wait_ge(ready, count)
                    for k in range(KE):
                        last = nc.tensor.matmul(to, w[:, k, g * P:(g + 1) * P], c[:, par, k, :],
                                                start=n == 0, stop=n == 3 * KE - 1)
                        n += 1
                last.then_inc(k_made, 1)

            def v_project(m, par, t, free):
                if free:
                    pe.wait_ge(v_ready, m)
                n = 0
                for c, w in ((c_hi, wv_hi), (c_hi, wv_lo), (c_lo, wv_hi)):
                    for k in range(KE):
                        last = nc.tensor.matmul(vp[:], c[:, par, k, t * P:(t + 1) * P], w[:, k, :],
                                                start=n == 0, stop=n == 3 * KE - 1)
                        n += 1
                last.then_inc(v_made, 1)

            def scores(n, par, t, g, free):
                if free:
                    pe.wait_ge(probs_ready, n - 1)
                for j in range(HG):
                    last = nc.tensor.matmul(sc[g % 2][:, j * L:(j + 1) * L],
                                            kst[0:3 * D, par, j, g, t * P:(t + 1) * P],
                                            qst[0:3 * D, j, g, :], start=True, stop=True)
                last.then_inc(scores_ready, 1)

            def weigh(tile, t, g):
                if g == 0:
                    pe.wait_ge(v_ready, tile + 1)
                pe.wait_ge(probs_ready, tile * G + g + 1)
                for j in range(HG):
                    h = g * HG + j
                    last = nc.tensor.matmul(acc[D * j:D * (j + 1), g, :], v[:, t % 2, h * D:(h + 1) * D],
                                            probs[:, t % 2, g, j * L:(j + 1) * L], start=False, stop=False,
                                            skip_group_check=True)
                if g == G - 1:
                    last.then_inc(probs_used, 1)

            k_project(0, 0, 0, k_first[0], False, before=(
                ((wk_hi_done, 1), (ctx_hi, 1)), ((wk_split, 1),), ((ctx_split, 1),)))
            for g in range(1, G):
                k_project(g, 0, g, k_first[g], False)
            pe.wait_ge(q_lo, HG)
            pe.wait_ge(q_dup, HG * 16)

            def first_stack(g):
                pe.wait_ge(k_lo, (g + 1) * HG)
                pe.wait_ge(k_dup0[g], 16)

            def zero_sums():
                pe.wait_ge(k_lo, G * HG)
                for b in range(G * L // 512):
                    nc.tensor.matmul(acc[:, 2 * b:2 * b + 2, :], zeros[:, 0:P], zeros[:], start=True, stop=True,
                                     skip_group_check=True)

            def last_chunk(tile0, par):
                def group_scores(n):
                    scores(tile0 * G + n, par, n // G, n % G, True)

                for n in range(2):
                    group_scores(n)
                for n in range(TC * G):
                    t, g = divmod(n, G)
                    if g == 0 and t < TC - 1:
                        v_project(tile0 + t + 1, par, t + 1, True)
                    if n + 2 < TC * G:
                        group_scores(n + 2)
                    weigh(tile0 + t, t, g)

            def one(c, par, first, k_next, split_next, load_next, looped):
                if not first:
                    pe.wait_ge(k_lo, (c + 1) * G * HG)
                    pe.wait_ge(k_dup, c * G)
                if not k_next:
                    return last_chunk(c * TC, par)
                for t in range(TC):
                    tile = c * TC + t
                    for g in (0, 1):
                        if first and t == 0:
                            first_stack(g)
                        scores(tile * G + g, par, t, g, not (first and t == 0))
                    if first and t == 0:
                        pe.wait_ge(wv_split, 1)
                        v_project(0, 0, 0, False)
                    if t == 0:
                        pe.wait_ge(ctx_split, c + 2)
                    k_project(tile + TC, 1 - par, t, kp[:], not (first and t == 0))
                    if first and t == 0:
                        zero_sums()
                    for g in (2, 3):
                        if first and t == 0:
                            first_stack(g)
                        scores(tile * G + g, par, t, g, True)
                    ahead = t + 1 if t < TC - 1 else 0
                    v_project(tile + 1, par if ahead else 1 - par, ahead, True)
                    for g in range(G):
                        weigh(tile, t, g)

            chunks(pe, one)
            pe.wait_ge(wo_loaded, 16)

            def transpose_norm(a):
                pe.wait_ge(xn1_ready, a + 1)
                for k in range(KE):
                    last = nc.tensor.transpose(sc[0][:, a * E + k * P:a * E + (k + 1) * P],
                                               keep["xn"][:, a, k * P:(k + 1) * P], ident[:])
                last.then_inc(xn1T_made, 1)

            def v_self(a, to):
                pe.wait_ge(x1_ready, a + 1)
                pe.wait_ge(xn1T_ready, a + 1)
                for k in range(KE):
                    last = nc.tensor.matmul(to[:], keep["xnT"][:, k, a * P:(a + 1) * P], next_weights[:, 0, k, :],
                                            start=k == 0, stop=k == KE - 1)
                last.then_inc(v1_made, 1)

            for a, to in enumerate((kp, vp)):
                for g in range(G):
                    if a == 1 and g == G - 1:
                        transpose_norm(0)
                    pe.wait_ge(o_saved, g + 1)
                    last = nc.tensor.matmul(to[:], oT[:, g, a * P:(a + 1) * P], wo_sb[:, g, :],
                                            start=g == 0, stop=g == G - 1)
                last.then_inc(o_projected, 1)
            pe.wait_ge(keep["wv_loaded"], 16)
            v_self(0, kp)
            transpose_norm(1)
            v_self(1, vp)


def self_attention(nc, bqk, wn, bn, bo, scales, s3, w_all, keep):
    ident, x1, x2, x_hi, x_lo = keep["ident"], keep["x1"], keep["x2"], keep["x_hi"], keep["x_lo"]
    raw, raw_loaded, w_hi, w_lo = keep["raw"], keep["raw_loaded"], keep["w_hi"], keep["w_lo"]
    w_rounded, w_split = keep["w_rounded"], keep["w_split"]
    SW = L + P
    with ExitStack() as stack:
        def sb(name, shape, dt=F32):
            return stack.enter_context(nc.sbuf_tensor(name, shape, dt))

        def sem(name):
            return stack.enter_context(nc.semaphore(name))

        wq_sb, wk_sb, wo_sb = (keep["weights"][1][:, i, :, :] for i in range(1, 4))
        wn_sb, bqk_sb = sb("wn_sb", [P, KE, H]), sb("bqk_sb", [P, 2 * KE])
        bo_sb, bn_sb, bn_neg = sb("bo_sb", [P, E]), sb("bn_sb", [H, 1]), sb("bn_neg", [H, 1])
        xnT = keep["xnT"]
        qT = sb("qT", [P, G, L])
        v = keep["v"]
        kT = keep["rows"][1][:, 3, :, :]
        xn = kT.rearrange("p g l -> p (g l)").rearrange("p (a n) -> p a n", a=LT)
        n_inv, heads, n_rows = sb("n_inv", [H, L]), sb("heads", [H, G, P]), sb("n_rows", [P, G, L])
        ones, inexact, differs = sb("ones", [P, 1]), sb("inexact", [P, 1]), sb("differs", [P, PIECE])
        mask, st, cT = sb("mask", [P, SW]), sb("st", [P, H, SW]), sb("cT", [P, G, L])
        stats, mv = sb("ln2_stats", [P, LT, 6]), sb("ln2_mv", [P, LT, 4])
        qk_p = [stack.enter_context(nc.psum_tensor(f"qk_p{i}", [P, 2, L], F32)) for i in range(2)]
        st_p = stack.enter_context(nc.psum_tensor("st_p", [P, HG, 512], F32))
        xT_psum = stack.enter_context(nc.psum_tensor("xT_psum", [P, LT, E], F32))
        cx_p = xT_psum[:, :, :].rearrange("p a n -> p (a n)").rearrange("p (g l) -> p g l", g=G)
        rows_p, n_p = cx_p, st_p[0:H, 0, 0:L]

        def norm_of(a):
            return xT_psum[:, a, :].rearrange("p (k l) -> p k l", k=KE)

        bias_loaded = sem("bias_ld")
        mask_one, heads_one, heads_step, const_ready = (
            sem("mask_one"), sem("heads_one"), sem("heads_step"), sem("const2_ready"))
        chain, var_ready, sd_ready, xn_ready = sem("chain2"), sem("var2"), sem("sd2"), sem("xn2_ready")
        n_made, bn_ready, n_ready, rows_made, rows_ready = (
            sem("n_made"), sem("bn_ready"), sem("n_ready"), sem("rows_made"), sem("rows_ready"))
        qk_made, q_ready, k_ready = sem("qk_made"), sem("qs_ready"), sem("ks_ready")
        st_made, st_ready, cx_made, cx_ready = sem("st_made"), sem("st_ready"), sem("cx_made"), sem("cx_ready")
        differs_ready, inexact_ready = sem("differs_ready"), sem("inexact_ready")
        ones_ready, inexact_made = sem("ones_ready"), sem("inexact_made")
        x1b_ready, out_made, x2_ready = sem("x1b_ready"), sem("out_made"), sem("x2_ready")
        xT_made, x_rounded = sem("xT_made"), sem("x_rounded")
        block = stack.enter_context(nc.Block())

        @block.sync
        def _(sp):
            sp.dma_start(wn_sb[:], wn).then_inc(bias_loaded, 16)
            sp.dma_start(bqk_sb[:], bqk).then_inc(bias_loaded, 16)
            sp.dma_start(bn_sb[:], bn).then_inc(bias_loaded, 16)
            sp.dma_start(bo_sb[:], bo.partition_broadcast(P)).then_inc(bias_loaded, 16)
            for q in range(RING):
                sp.dma_start(raw[:, q, :], w_all[q]).then_inc(raw_loaded[q], 16)
            for i, s in enumerate(scales):
                sp.dma_start(keep["scales"][:, i, :], s).then_inc(keep["scales_loaded"], 16)
            sp.dma_start(keep["s3"][:], s3.partition_broadcast(P)).then_inc(keep["scales_loaded"], 16)

        @block.gpsimd
        def _(pool):
            nc.gpsimd.memset(ones[:], 1.0).then_inc(ones_ready, 1)
            nc.gpsimd.memset(heads[:], 1.0).then_inc(heads_one, 1)
            nc.gpsimd.memset(mask[:], 1.0).then_inc(mask_one, 1)
            pool.wait_ge(heads_one, 1)
            nc.gpsimd.affine_select(out=heads[:], in_=heads[:], compare_op=ALU.is_ge, fill=0.0, base=0,
                                    pattern=[[P, G], [1, P]], channel_multiplier=-D).then_inc(heads_step, 1)
            pool.wait_ge(heads_step, 1)
            nc.gpsimd.affine_select(out=heads[:], in_=heads[:], compare_op=ALU.is_ge, fill=0.0, base=D - 1,
                                    pattern=[[-P, G], [-1, P]], channel_multiplier=D).then_inc(const_ready, 1)
            pool.wait_ge(mask_one, 1)
            for at in (0, L):
                nc.gpsimd.affine_select(out=mask[:, at:at + P], in_=mask[:, at:at + P], compare_op=ALU.is_ge,
                                        fill=0.0, base=0, pattern=[[1, P]],
                                        channel_multiplier=-1).then_inc(const_ready, 1)

        @block.scalar
        def _(act):
            act.wait_ge(bias_loaded, 16 * 4)
            for g in range(G):
                act.wait_ge(qk_made, g + 1)
                nc.scalar.activation(qT[:, g, :], qk_p[g % 2][:, 0, :], ACT.Identity,
                                     bias=bqk_sb[:, g:g + 1]).then_inc(q_ready, 1)
                if g == 0:
                    act.wait_ge(bn_ready, 1)
                    act.wait_ge(n_made, 1)
                    nc.scalar.activation(n_inv[:], n_p, ACT.Exp, bias=bn_neg[:], scale=-1.0).then_inc(n_ready, 1)
                    table(nc, keep, ACT.Sqrt)
                if 1 <= g <= AHEAD:
                    act.wait_ge(raw_loaded[g - 1], 16)
                    nc.scalar.activation(w_hi[:, g - 1, :], raw[:, g - 1, :], ACT.Copy).then_inc(w_rounded, 1)
            roots(nc, act, mv, var_ready, sd_ready, 0)
            for a in range(LT):
                act.wait_ge(xT_made, a + 1)
                nc.scalar.activation(x_hi[:, :, a * P:(a + 1) * P], norm_of(a), ACT.Copy).then_inc(x_rounded, 1)

        @block.vector
        def _(dve):
            dve.wait_ge(bias_loaded, 16 * 4)
            nc.vector.tensor_scalar_mul(bn_neg[:], bn_sb[:], -1.0).then_inc(bn_ready, 1)
            def keys(g):
                dve.wait_ge(q_ready, g + 1)
                nc.vector.tensor_scalar_add(kT[:, g, :], qk_p[g % 2][:, 1, :],
                                            bqk_sb[:, KE + g:KE + g + 1]).then_inc(k_ready, 1)

            def masked(g):
                dve.wait_ge(st_made, g + 1)
                nc.vector.tensor_tensor(st[:, g * HG:(g + 1) * HG, :], st_p[:, :, 0:SW],
                                        mask[:].unsqueeze(1).to_broadcast([P, HG, SW]), ALU.mult).then_inc(st_ready, 1)

            def weighed(g):
                dve.wait_ge(cx_made, g + 1)
                nc.vector.tensor_tensor(cT[:, g, :], cx_p[:, g, :], n_rows[:, g, :], ALU.mult).then_inc(cx_ready, 1)

            def w_rest(q):
                dve.wait_ge(w_rounded, q + 1)
                nc.vector.tensor_tensor(w_lo[:, q, :], raw[:, q, :], f32(w_hi[:, q, :]),
                                        ALU.subtract).then_inc(w_split, 1)

            keys(0)
            for a in range(LT):
                nc.vector.tensor_tensor(x1[:, a, :], x1[:, a, :], bo_sb[:], ALU.add).then_inc(x1b_ready, 1)
            keys(1)
            dve.wait_ge(rows_made, 1)
            nc.vector.tensor_copy(n_rows[:], rows_p).then_inc(rows_ready, 1)
            dve.wait_ge(rows_ready, 1)
            dve.wait_ge(const_ready, 3)
            masked(0)
            keys(2)
            w_rest(0)
            masked(1)
            nc.vector.tensor_scalar(differs[:], keep["exact"][:], float(PIECES), None,
                                    ALU.not_equal).then_inc(differs_ready, 1)
            dve.wait_ge(differs_ready, 1)
            nc.vector.tensor_reduce(inexact[:], differs[:], mybir.AxisListType.X, ALU.max).then_inc(inexact_ready, 1)
            keys(3)
            masked(2)
            dve.wait_ge(cx_made, 2)
            weighed(0)
            weighed(1)
            masked(3)
            dve.wait_ge(cx_made, G)
            weighed(2)
            weighed(3)
            dve.wait_ge(inexact_made, 1)
            nc.vector.tensor_copy(keep["any_inexact"][:], st_p[0:1, 0, 0:1]).then_inc(keep["inexact_ready"], 1)
            dve.wait_ge(x1b_ready, LT)
            w_rest(1)
            norm = Layernorm(nc, dve, x2, xn, stats, mv, Chain(dve, chain), var_ready, sd_ready, 0, xn_ready)
            for a in range(LT):
                dve.wait_ge(out_made, a + 1)
                nc.vector.tensor_tensor(x2[:, a, :], qk_p[a][:].rearrange("p b n -> p (b n)"), x1[:, a, :],
                                        ALU.add).then_inc(x2_ready, 1)
                dve.wait_ge(x2_ready, a + 1)
                norm.moments(a)
                norm.normalised(a)
            for a in range(LT):
                dve.wait_ge(x_rounded, a + 1)
                nc.vector.tensor_tensor(x_lo[:, :, a * P:(a + 1) * P], norm_of(a), f32(x_hi[:, :, a * P:(a + 1) * P]),
                                        ALU.subtract).then_inc(keep["x_split"], 1)

        @block.tensor
        def _(pe):
            pe.wait_ge(keep["wqk_loaded"], 32)

            def queries_keys(g):
                if g > 1:
                    pe.wait_ge(q_ready, g - 1)
                    pe.wait_ge(k_ready, g - 1)
                for b in range(2):
                    for k in range(KE):
                        last = nc.tensor.matmul(qk_p[g % 2][:, b, :], (wq_sb, wk_sb)[b][:, k, g * P:(g + 1) * P],
                                                xnT[:, k, :], start=k == 0, stop=k == KE - 1)
                last.then_inc(qk_made, 1)

            def scores(g):
                pe.wait_ge(q_ready, g + 1)
                pe.wait_ge(k_ready, g + 1)
                if g:
                    pe.wait_ge(st_ready, g)
                else:
                    pe.wait_ge(n_ready, 1)
                for j in range(HG):
                    rows = slice(D * j, D * (j + 1))
                    nc.tensor.matmul(st_p[:, j, 0:L], kT[rows, g, 0:P], qT[rows, g, :], start=True, stop=True)
                    last = nc.tensor.matmul(st_p[:, j, L:SW], kT[rows, g, P:L], qT[rows, g, P:L],
                                            start=True, stop=True)
                last.then_inc(st_made, 1)

            def weigh(g):
                pe.wait_ge(st_ready, g + 1)
                if not g:
                    pe.wait_ge(rows_ready, 1)
                for s in range(LT):
                    for j in range(HG):
                        h = g * HG + j
                        last = nc.tensor.matmul(cx_p[D * j:D * (j + 1), g, s * P:L], v[:, s, h * D:(h + 1) * D],
                                                st[:, h, s * L:s * L + L - s * P], start=s == 0, stop=s == LT - 1)
                last.then_inc(cx_made, 1)

            queries_keys(0)
            pe.wait_ge(bias_loaded, 16 * 4)
            for k in range(KE):
                last = nc.tensor.matmul(n_p, wn_sb[:, k, :], xnT[:, k, :], start=k == 0, stop=k == KE - 1)
            last.then_inc(n_made, 1)
            queries_keys(1)
            pe.wait_ge(n_ready, 1)
            pe.wait_ge(const_ready, 1)
            for g in range(G):
                last = nc.tensor.matmul(rows_p[:, g, :], heads[:, g, :], n_inv[:], start=True, stop=True)
            last.then_inc(rows_made, 1)
            scores(0)
            queries_keys(2)
            scores(1)
            queries_keys(3)
            scores(2)
            weigh(0)
            weigh(1)
            scores(3)
            weigh(2)
            pe.wait_ge(keep["wo_loaded"], 16)
            pe.wait_ge(q_ready, G)
            pe.wait_ge(k_ready, G)

            def project(a, groups):
                for g in groups:
                    pe.wait_ge(cx_ready, g + 1)
                    last = nc.tensor.matmul(qk_p[a][:], cT[:, g, a * P:(a + 1) * P], wo_sb[:, g, :],
                                            start=g == 0, stop=g == G - 1)
                if g == G - 1:
                    last.then_inc(out_made, 1)

            project(0, (0, 1))
            weigh(3)
            project(1, (0,))
            pe.wait_ge(ones_ready, 1)
            pe.wait_ge(inexact_ready, 1)
            nc.tensor.matmul(st_p[0:1, 0, 0:1], inexact[:], ones[:], start=True, stop=True).then_inc(inexact_made, 1)
            project(0, (2, 3))
            project(1, (1, 2, 3))
            keep_clock(nc, keep, st_p[:, 1, :], 4)

            def transpose_norm(a):
                pe.wait_ge(xn_ready, a + 1)
                for k in range(KE):
                    last = nc.tensor.transpose(xT_psum[:, a, k * P:(k + 1) * P], xn[:, a, k * P:(k + 1) * P], ident[:])
                last.then_inc(xT_made, 1)

            transpose_norm(0)
            keep_clock(nc, keep, st_p[:, 1, :], 9)
            transpose_norm(1)
            keep_clock(nc, keep, st_p[:, 1, :], 6)


U1 = 2 * HID // (2 * 2 * P)
UH = KH
U3 = KH // 4
RING = 4
AHEAD = 2
UNITS = U1 + 2 * UH + U3
PIECE = 512
PIECES = UNITS * UNIT // PIECE
FIRST = {1: 0, 2: U1, 3: U1 + UH, 4: U1 + 2 * UH}
TILE0 = {1: 0, 2: KH, 3: 2 * KH}
assert not any(n % RING for n in FIRST.values()) and U3 == RING


def units(engine, one):
    for i in range(U1 // RING):
        for q in range(RING):
            one(1, i, q)
    for layer in (2, 3):
        with engine.Fori(0, UH // RING) as i:
            for q in range(RING):
                one(layer, i, q)
    for q in range(RING):
        one(4, 0, q)


def mlp(nc, w_all, out, keep):
    x2, raw, raw_loaded = keep["x2"], keep["raw"], keep["raw_loaded"]
    w_hi, w_lo, w_rounded, w_split = keep["w_hi"], keep["w_lo"], keep["w_rounded"], keep["w_split"]
    with ExitStack() as stack:
        def sb(name, shape, dt=F32):
            return stack.enter_context(nc.sbuf_tensor(name, shape, dt))

        def sem(name):
            return stack.enter_context(nc.semaphore(name))

        lent = [keep["weights"][0][:, 2 * i:2 * i + 2, :, :].rearrange("p a k n -> p (a k n)") for i in range(2)]
        h_hi0, h_lo0 = (w.rearrange("p (k l) -> p k l", k=KH) for w in lent)
        h_hi = [h_hi0, keep["rows"][0][:, :, :, :].rearrange("p j g l -> p (j g) l")]
        h_lo = [h_lo0, sb("h_lo1", [P, KH, L], F32R)]
        hf, gate = sb("hf", [P, 2, L]), sb("gate", [P, 2, L])
        scale, s3_sb, y = keep["scales"], keep["s3"], sb("y", [P, LT, E])
        ps = [stack.enter_context(nc.psum_tensor(f"ps{i}", [P, 2, L], F32)) for i in range(4)]
        py = [stack.enter_context(nc.psum_tensor(f"py{i}", [P, E], F32)) for i in range(LT)]

        scales_loaded, stored = keep["scales_loaded"], sem("stored")
        sums_ready, act_ready, hf_ready = sem("sums_ready"), sem("act_ready"), sem("hf_ready")
        h_rounded, h_ready = sem("h_rounded"), sem("h_ready")
        y_step, y_ready = sem("y_step"), sem("y_ready")
        y_made = sem("y_made")
        block = stack.enter_context(nc.Block())

        @block.sync
        def _(sp):
            def one(layer, i, q):
                if layer == 1 and i == 0:
                    return
                sp.wait_ge(w_split, i * RING + (FIRST[layer] + q - RING + 1))
                sp.dma_start(raw[:, q, :], w_all[i * RING + (FIRST[layer] + q)]).then_inc(raw_loaded[q], 16)

            units(sp, one)
            for a in range(LT):
                sp.wait_ge(y_ready, a + 1)
                sp.dma_start(out[0, a * P:(a + 1) * P, :], y[:, a, :]).then_inc(stored, 16)
            sp.wait_ge(stored, 16 * LT)

        @block.scalar
        def _(act):
            table(nc, keep, ACT.Silu)
            act.wait_ge(scales_loaded, 16 * 5)

            def w_round(layer, i, q):
                at = (q + AHEAD) % RING
                act.wait_ge(raw_loaded[at], i * 16 + 16 * (FIRST[layer] // RING + (q + AHEAD) // RING + 1))
                u = i * RING + (FIRST[layer] + q + AHEAD)
                if layer == 1 and u >= RING:
                    act.wait_ge(sums_ready, 2 * (u - RING + 1))
                elif layer > 1:
                    act.wait_ge(sums_ready, u + (U1 - RING + 1))
                nc.scalar.activation(w_hi[:, at, :], raw[:, at, :], ACT.Copy).then_inc(w_rounded, 1)

            def one(layer, i, q):
                if not (layer == 4 and q + AHEAD >= U3):
                    w_round(layer, i, q)
                if layer == 1:
                    for n in (2 * (i * RING + q), 2 * (i * RING + q) + 1):
                        act.wait_ge(sums_ready, n + 1)
                        if n >= 2:
                            act.wait_ge(hf_ready, n - 1)
                        nc.scalar.activation(gate[:, n % 2, :], ps[n % 4][:, 0, :], ACT.Silu,
                                             scale=scale[:, 0, n:n + 1]).then_inc(act_ready, 1)
                elif layer < 4:
                    n = i * RING + (TILE0[layer] + q)
                    act.wait_ge(sums_ready, n + 1)
                    act.wait_ge(h_ready, n - 1)
                    nc.scalar.activation(hf[:, q % 2, :], ps[q][:, 0, :], ACT.Gelu,
                                         scale=scale[:, layer, bass.ds(i * RING + q, 1)]).then_inc(act_ready, 1)

            units(act, one)

        @block.vector
        def _(dve):
            dve.wait_ge(scales_loaded, 16 * 5)

            def hidden(exact):
                def w_rest(layer, i, q):
                    at = (q + AHEAD) % RING
                    dve.wait_ge(w_rounded, i * RING + (FIRST[layer] + q + AHEAD + 1))
                    n = 1 if exact else UNIT
                    nc.vector.tensor_tensor(w_lo[:, at, 0:n], raw[:, at, 0:n], f32(w_hi[:, at, 0:n]),
                                            ALU.subtract).then_inc(w_split, 1)

                def h_split(n, o, slot, to):
                    nc.vector.tensor_copy(h_hi[to][:, bass.ds(o, 1), :], hf[:, slot:slot + 1, :]).then_inc(h_rounded, 1)
                    dve.wait_ge(h_rounded, n + 1)
                    nc.vector.tensor_tensor(h_lo[to][:, bass.ds(o, 1), :], hf[:, slot:slot + 1, :],
                                            f32(h_hi[to][:, bass.ds(o, 1), :]), ALU.subtract).then_inc(h_ready, 1)

                def one(layer, i, q):
                    if not (layer == 4 and q + AHEAD >= U3):
                        w_rest(layer, i, q)
                    if layer == 1:
                        for n in (2 * (i * RING + q), 2 * (i * RING + q) + 1):
                            dve.wait_ge(act_ready, n + 1)
                            if n >= 2:
                                dve.wait_ge(h_ready, n - 1)
                            nc.vector.scalar_tensor_tensor(out=hf[:, n % 2, :], in0=ps[n % 4][:, 1, :],
                                                           scalar=scale[:, 1, n:n + 1], in1=gate[:, n % 2, :],
                                                           op0=ALU.mult, op1=ALU.mult).then_inc(hf_ready, 1)
                            dve.wait_ge(hf_ready, n + 1)
                            h_split(n, n, n % 2, 0)
                    elif layer < 4:
                        n = i * RING + (TILE0[layer] + q)
                        dve.wait_ge(act_ready, n + 1)
                        h_split(n, i * RING + q, q % 2, layer % 2 ^ 1)

                units(dve, one)

            dve.wait_ge(keep["inexact_ready"], 1)
            count = nc.vector.value_load(keep["any_inexact"][:], min_val=0, max_val=P)
            with dve.If(count > 0):
                hidden(exact=False)
            with dve.Else():
                hidden(exact=True)
            for a in range(LT):
                dve.wait_ge(y_made, a + 1)
                nc.vector.tensor_tensor(y[:, a, :], py[a][:], s3_sb[:], ALU.mult).then_inc(y_step, 1)
                dve.wait_ge(y_step, a + 1)
                nc.vector.tensor_tensor(y[:, a, :], y[:, a, :], x2[:, a, :], ALU.add).then_inc(y_ready, 1)

        @block.tensor
        def _(pe):
            keep_clock(nc, keep, py[0][:], 4)
            pe.wait_ge(keep["x_split"], LT)

            def multiply(exact):
                def terms(w_hi, w_lo, x_hi, x_lo):
                    return ((w_hi, x_hi), (w_hi, x_lo)) if exact else ((w_hi, x_hi), (w_lo, x_hi), (w_hi, x_lo))

                passes = 2 if exact else 3

                def one(layer, i, q):
                    pe.wait_ge(w_split, i * RING + (FIRST[layer] + q + 1))
                    if layer == 1:
                        hi = w_hi[:, q, :].rearrange("p (w o k n) -> p w o k n", w=2, o=2, k=KE)
                        lo = w_lo[:, q, :].rearrange("p (w o k n) -> p w o k n", w=2, o=2, k=KE)
                        for o in range(2):
                            n = 2 * (i * RING + q) + o
                            if n >= 4:
                                pe.wait_ge(hf_ready, n - 3)
                            for w in range(2):
                                m = 0
                                for wt, x in terms(hi, lo, keep["x_hi"], keep["x_lo"]):
                                    for k in range(KE):
                                        last = nc.tensor.matmul(ps[n % 4][:, w, :], wt[:, w, o, k, :], x[:, k, :],
                                                                start=m == 0, stop=m == passes * KE - 1)
                                        m += 1
                            last.then_inc(sums_ready, 1)
                    elif layer < 4:
                        hi = w_hi[:, q, :].rearrange("p (k n) -> p k n", k=KH)
                        lo = w_lo[:, q, :].rearrange("p (k n) -> p k n", k=KH)
                        src = layer % 2
                        pe.wait_ge(act_ready, i * RING + (TILE0[layer] + q - 3))
                        m = 0
                        for tiles in (range(KH - 2), range(KH - 2, KH)):
                            pe.wait_ge(h_ready, TILE0[layer] - KH + tiles.stop)
                            for wt, x in terms(hi, lo, h_hi[src], h_lo[src]):
                                for k in tiles:
                                    last = nc.tensor.matmul(ps[q][:, 0, :], wt[:, k, :], x[:, k, :],
                                                            start=m == 0, stop=m == passes * KH - 1)
                                    m += 1
                        last.then_inc(sums_ready, 1)
                    else:
                        hi = w_hi[:, q, :].rearrange("p (k n) -> p k n", k=4)
                        lo = w_lo[:, q, :].rearrange("p (k n) -> p k n", k=4)
                        pe.wait_ge(h_ready, 2 * KH + 4 * q + 4)
                        for a in range(LT):
                            rows = slice(a * P, (a + 1) * P)
                            m = 0
                            for wt, x in terms(hi, lo, h_hi[0], h_lo[0]):
                                for k in range(4):
                                    last = nc.tensor.matmul(py[a][:], x[:, 4 * q + k, rows], wt[:, k, :],
                                                            start=q == 0 and m == 0,
                                                            stop=q == U3 - 1 and m == passes * 4 - 1)
                                    m += 1
                            if q == U3 - 1:
                                last.then_inc(y_made, 1)

                units(pe, one)

            pe.wait_ge(keep["inexact_ready"], 1)
            count = nc.tensor.value_load(keep["any_inexact"][:], min_val=0, max_val=P)
            with pe.If(count > 0):
                multiply(exact=False)
            with pe.Else():
                multiply(exact=True)


def build(nc, x, ctxT, wqT, wkT, wvT, woT, wqk, bqk, wv, bv, wn, bn, wo, bo,
          w_all, s1, s2, sh1, sh2, s3, out):
    with ExitStack() as stack:
        def sb(name, shape, dt=F32):
            return stack.enter_context(nc.sbuf_tensor(name, shape, dt))

        def sem(name):
            return stack.enter_context(nc.semaphore(name))

        def two_types(name, shape):
            with nc.sbuf_tensor(f"{name}_r", shape, F32R) as as_f32r:
                pass
            as_f32 = sb(name, shape)
            return as_f32r, as_f32

        keep = {"ident": sb("ident", [P, P]), "x1": sb("x1", [P, LT, E]), "exact": sb("exact", [P, PIECE]),
                "zeros": sb("zeros", [P, 512], BF16), "one": sb("one", [P, 8]), "tables": 0,
                "weights": two_types("weights", [P, 4, KE, E]), "rows": two_types("rows", [P, HG, G, L]),
                "wv_loaded": sem("wvs_ld"), "wqk_loaded": sem("wqks_ld"), "wo_loaded": sem("wos_ld")}
        rows = keep["rows"][1]
        keep["xn"] = rows[:, 0, :, :].rearrange("p g l -> p (g l)").rearrange("p (a n) -> p a n", a=LT)
        keep["xnT"] = rows[:, 1, :, :]
        keep["v"] = rows[:, 2, :, :].rearrange("p g l -> p (g l)").rearrange("p (a n) -> p a n", a=LT)
        cross_attention(nc, x, ctxT, wqT, wkT, wvT, woT, wqk, wv, bv, wo, w_all, keep)
        keep |= {"any_inexact": sb("any_inexact", [1, 1], mybir.dt.int32), "inexact_ready": sem("any_inexact_ready"),
                 "x2": sb("x2", [P, LT, E]), "raw": sb("w_raw", [P, RING, UNIT]),
                 "w_hi": sb("w_hi", [P, RING, UNIT], F32R), "w_lo": sb("w_lo", [P, RING, UNIT], F32R),
                 "scales": sb("scales", [P, 4, KH]), "s3": sb("s3_sb", [P, E]), "scales_loaded": sem("scales_ld"),
                 "x_hi": keep["rows"][0][:, 0, :, :], "x_lo": keep["rows"][0][:, 1, :, :], "x_split": sem("x_split"),
                 "raw_loaded": [sem(f"raw_loaded{q}") for q in range(RING)],
                 "w_rounded": sem("w_rounded"), "w_split": sem("w_split")}
        self_attention(nc, bqk, wn, bn, bo, (s1, s2, sh1, sh2), s3, w_all, keep)
        mlp(nc, w_all, out, keep)


def kernel(**inputs):
    from concourse import bacc
    from concourse.bass_utils import run_bass_kernel_spmd

    a = {k: np.asarray(v) for k, v in inputs.items()}

    def rows_split(w):
        return w.reshape(-1, P, w.shape[1]).transpose(1, 0, 2)

    def out_tiles(w):
        return w.reshape(w.shape[0] // P, P, w.shape[1] // P, P).transpose(0, 3, 2, 1)

    w1, w2 = (out_tiles(a[f"L0_ffn_{n}_w"]).reshape(U1, 2, P, KE * P).transpose(0, 2, 1, 3) for n in ("w1", "w2"))
    arrays = {
        "x": a["x"],
        "ctxT": a["ctx_1024"][0].reshape(NC, CH, KE, P).transpose(0, 3, 2, 1),
        "wqT": rows_split(a["L0_xattn_Wq"].T),
        "wkT": rows_split(a["L0_xattn_Wk"].T),
        "wvT": rows_split(a["L0_xattn_Wv"].T),
        "woT": rows_split(a["L0_xattn_Wo"].T),
        "wqk": rows_split(a["L0_attn_Wqk"]),
        "bqk": a["L0_attn_bqk"].reshape(2 * KE, P).T,
        "wv": rows_split(a["L0_attn_Wv"]), "bv": a["L0_attn_bv"],
        "wn": rows_split(a["L0_attn_Wn"]), "bn": a["L0_attn_bn"].reshape(H, 1),
        "wo": rows_split(a["L0_attn_Wo"]), "bo": a["L0_attn_bo"],
        "w_all": np.concatenate([
            np.stack([w1, w2], axis=2).reshape(U1, P, UNIT),
            out_tiles(a["L0_ffn_h1_w"]).reshape(UH, P, UNIT),
            out_tiles(a["L0_ffn_h2_w"]).reshape(UH, P, UNIT),
            a["L0_ffn_w3_w"].T.reshape(U3, 4, P, E).transpose(0, 2, 1, 3).reshape(U3, P, UNIT)]),
        "s1": a["L0_ffn_w1_s"].reshape(KH, P).T, "s2": a["L0_ffn_w2_s"].reshape(KH, P).T,
        "sh1": a["L0_ffn_h1_s"].reshape(KH, P).T, "sh2": a["L0_ffn_h2_s"].reshape(KH, P).T,
        "s3": a["L0_ffn_w3_s"],
    }
    arrays = {f"{k}_dram": np.ascontiguousarray(v) for k, v in arrays.items()}
    nc = bacc.Bacc("TRN2", target_bir_lowering=False, num_devices=1)
    aps = [nc.dram_tensor(k, v.shape, mybir.dt.from_np(v.dtype), kind="ExternalInput").ap()
           for k, v in arrays.items()]
    out = nc.dram_tensor("out_dram", (1, L, E), F32, kind="ExternalOutput").ap()
    build(nc, *aps, out)
    result = run_bass_kernel_spmd(nc, [arrays], core_ids=[0])
    return result.results[0]["out_dram"]
```
